# Optimizing a Trainium2 kernel written in Bass

```python
import numpy as np
import jax
import jax.numpy as jnp

def _softmax(x, axis=-1):
    return jax.nn.softmax(x, axis=axis)

def _gelu(x):
    return jax.nn.gelu(x, approximate=True)

def _silu(x):
    return jax.nn.silu(x)

def _sigmoid(x):
    return jax.nn.sigmoid(x)

def _layernorm(x, axis=-1, eps=1e-05):
    m = jnp.mean(x, axis=axis, keepdims=True)
    v = jnp.var(x, axis=axis, keepdims=True)
    return (x - m) / jnp.sqrt(v + eps)

def _scatter_add(tgt, idx, src, axis=0):
    return tgt.at[idx].add(src)

def _segment_sum(src, seg, n):
    return jax.ops.segment_sum(src, seg, n)
kernel_name = 'mk_seq_preln_d1_jaxref_r8_a8774b'

def setup_inputs(seed: int=0):
    np.random.seed(seed)
    _w = jnp.asarray

    def _L0_attn_setup():
        import jax, jax.numpy as jnp
        import numpy as np
        import math
        B, L, D, N = (8, 512, 128, 16)
        key = jax.random.key(seed)
        k1, k2, k3, k4, k5, k6 = jax.random.split(key, 6)
        return {'x': jax.random.normal(k1, (B, L, D), dtype=jnp.float32), 'delta': jax.random.normal(k2, (D, N, 1), dtype=jnp.float32), 'alpha': jax.random.normal(k3, (D, N, 1), dtype=jnp.float32), 'beta': jax.random.normal(k4, (D, N, 1), dtype=jnp.float32), 'gamma': jax.random.normal(k5, (D, N), dtype=jnp.float32), 'omega': jax.random.normal(k6, (D,), dtype=jnp.float32)}
    _L0_attn_in = _L0_attn_setup()

    def _L0_ffn_setup():
        import jax, jax.numpy as jnp
        import numpy as np
        DIM = 128
        DEPTH = 2
        HEADS = 8
        DIM_HEAD = 64
        WINDOW = 64
        INNER = HEADS * DIM_HEAD
        HID = int(DIM * 4 * 2 / 3)
        B, N = (2, 1024)
        QK_SCALE = 8.0

        def shift_token(t):
            t1, t2 = jnp.split(t, 2, axis=-1)
            t2 = jnp.pad(t2, ((0, 0), (1, 0), (0, 0)))[:, :-1]
            return jnp.concatenate([t1, t2], axis=-1)

        def l2norm(t):
            return t / jnp.clip(jnp.linalg.norm(t, axis=-1, keepdims=True), 1e-12)

        def rotate_half(x):
            x1, x2 = jnp.split(x, 2, axis=-1)
            return jnp.concatenate([-x2, x1], axis=-1)

        def rotary_xpos(q, k):
            n = q.shape[-2]
            half_idx = jnp.arange(0, DIM_HEAD, 2, dtype=jnp.float32)
            inv_freq = 1.0 / 10000.0 ** (half_idx / DIM_HEAD)
            t = jnp.arange(n, dtype=jnp.float32)
            freqs = t[:, None] * inv_freq[None, :]
            freqs = jnp.concatenate([freqs, freqs], axis=-1)
            base = (half_idx + 0.4 * DIM_HEAD) / (1.4 * DIM_HEAD)
            power = (t - n // 2) / float(WINDOW // 2)
            scale = base[None, :] ** power[:, None]
            scale = jnp.concatenate([scale, scale], axis=-1)
            cos, sin = (jnp.cos(freqs), jnp.sin(freqs))
            q = q * cos * scale + rotate_half(q) * sin * scale
            k = k * cos / scale + rotate_half(k) * sin / scale
            return (q, k)

        def local_attention(q, k, v):
            b, h, n, d = q.shape
            w = n // WINDOW
            bq = q.reshape(b, h, w, WINDOW, d) * QK_SCALE
            bk = k.reshape(b, h, w, WINDOW, d)
            bv = v.reshape(b, h, w, WINDOW, d)

            def look_around(t):
                p = jnp.pad(t, ((0, 0), (0, 0), (1, 0), (0, 0), (0, 0)))
                return jnp.concatenate([p[:, :, :w], p[:, :, 1:]], axis=3)
            bk, bv = (look_around(bk), look_around(bv))
            bt = jnp.arange(n).reshape(w, WINDOW)
            btp = jnp.pad(bt, ((1, 0), (0, 0)), constant_values=-1)
            btk = jnp.concatenate([btp[:w], btp[1:]], axis=1)
            sim = jnp.einsum('bhwid,bhwjd->bhwij', bq, bk)
            i = bt[:, :, None]
            j = btk[:, None, :]
            mask = (i < j) | (i > j + WINDOW) | (j == -1)
            sim = jnp.where(mask, -jnp.finfo(sim.dtype).max, sim)
            attn = jax.nn.softmax(sim, axis=-1)
            out = jnp.einsum('bhwij,bhwjd->bhwid', attn, bv)
            return out.reshape(b, h, n, d)

        def _layer(x, wqkv, qs, ksc, wo, lg, lb, w1, b1, w2, b2):
            b, n, _ = x.shape
            h = shift_token(x)
            qkv = h @ wqkv
            q, k, v = jnp.split(qkv, 3, axis=-1)
            to_heads = lambda t: t.reshape(b, n, HEADS, DIM_HEAD).transpose(0, 2, 1, 3)
            q, k, v = (to_heads(q), to_heads(k), to_heads(v))
            q = l2norm(q) * qs
            k = l2norm(k) * ksc
            q, k = rotary_xpos(q, k)
            o = local_attention(q, k, v)
            o = o.transpose(0, 2, 1, 3).reshape(b, n, INNER)
            x = x + o @ wo
            h = shift_token(x)
            mu = h.mean(-1, keepdims=True)
            var = h.var(-1, keepdims=True)
            h = (h - mu) / jnp.sqrt(var + 1e-05) * lg + lb
            h = h @ w1 + b1
            a, g = jnp.split(h, 2, axis=-1)
            h = a * jax.nn.gelu(g, approximate=False)
            x = x + h @ w2 + b2
            return x
        key = jax.random.key(seed)
        ks = jax.random.split(key, 6)
        return {'x': jax.random.normal(ks[0], (B, N, DIM), jnp.float32), 'wqkv': jax.random.normal(ks[1], (DEPTH, DIM, 3 * INNER), jnp.float32) * 0.02, 'q_scale': jnp.ones((DEPTH, DIM_HEAD), jnp.float32), 'k_scale': jnp.ones((DEPTH, DIM_HEAD), jnp.float32), 'wo': jax.random.normal(ks[2], (DEPTH, INNER, DIM), jnp.float32) * 0.02, 'ln_g': jnp.ones((DEPTH, DIM), jnp.float32), 'ln_b': jnp.zeros((DEPTH, DIM), jnp.float32), 'w1': jax.random.normal(ks[3], (DEPTH, DIM, 2 * HID), jnp.float32) * 0.02, 'b1': jnp.zeros((DEPTH, 2 * HID), jnp.float32), 'w2': jax.random.normal(ks[4], (DEPTH, HID, DIM), jnp.float32) * 0.02, 'b2': jnp.zeros((DEPTH, DIM), jnp.float32)}
    _L0_ffn_in = _L0_ffn_setup()
    _d = {'L0_attn_x': _L0_attn_in['x'], 'L0_attn_delta': _L0_attn_in['delta'], 'L0_attn_alpha': _L0_attn_in['alpha'], 'L0_attn_beta': _L0_attn_in['beta'], 'L0_attn_gamma': _L0_attn_in['gamma'], 'L0_attn_omega': _L0_attn_in['omega'], 'L0_ffn_wqkv': _L0_ffn_in['wqkv'], 'L0_ffn_q_scale': _L0_ffn_in['q_scale'], 'L0_ffn_k_scale': _L0_ffn_in['k_scale'], 'L0_ffn_wo': _L0_ffn_in['wo'], 'L0_ffn_ln_g': _L0_ffn_in['ln_g'], 'L0_ffn_ln_b': _L0_ffn_in['ln_b'], 'L0_ffn_w1': _L0_ffn_in['w1'], 'L0_ffn_b1': _L0_ffn_in['b1'], 'L0_ffn_w2': _L0_ffn_in['w2'], 'L0_ffn_b2': _L0_ffn_in['b2']}
    _x0 = _d['L0_attn_x']
    _d['L0_attn_x'] = jax.random.normal(jax.random.fold_in(jax.random.key(seed), 1), (16, 512, 128), dtype=_x0.dtype)
    del _x0
    return _d

def reference(L0_attn_x, L0_attn_delta, L0_attn_alpha, L0_attn_beta, L0_attn_gamma, L0_attn_omega, L0_ffn_wqkv, L0_ffn_q_scale, L0_ffn_k_scale, L0_ffn_wo, L0_ffn_ln_g, L0_ffn_ln_b, L0_ffn_w1, L0_ffn_b1, L0_ffn_w2, L0_ffn_b2):

    def _L0_attn_ref(x, delta, alpha, beta, gamma, omega):
        import jax, jax.numpy as jnp
        import numpy as np
        import math
        B, L, D, N = (8, 512, 128, 16)
        b, l, d = x.shape
        n_state = gamma.shape[-1]
        scale = math.sqrt(1.0 / n_state)
        residual = x * omega
        xt = jnp.swapaxes(x, -1, -2)
        p = jax.nn.sigmoid(delta)
        a = jax.nn.sigmoid(alpha)
        q = 1.0 - p * a
        t = jnp.arange(l, dtype=x.dtype)
        vander = t[None, None, :] * jnp.log(q)
        kernel = p * beta * jnp.exp(vander)
        k = jnp.einsum('dnl,dn->dl', kernel, gamma * scale)
        n_fft = 2 * l
        k_f = jnp.fft.rfft(k, n=n_fft)
        x_f = jnp.fft.rfft(xt, n=n_fft)
        out = jnp.fft.irfft(x_f * k_f, n=n_fft)[..., :l]
        return jnp.swapaxes(out, -1, -2) + residual

    def _L0_ffn_ref(x, wqkv, q_scale, k_scale, wo, ln_g, ln_b, w1, b1, w2, b2):
        import jax, jax.numpy as jnp
        import numpy as np
        DIM = 128
        DEPTH = 2
        HEADS = 8
        DIM_HEAD = 64
        WINDOW = 64
        INNER = HEADS * DIM_HEAD
        HID = int(DIM * 4 * 2 / 3)
        B, N = (2, 1024)
        QK_SCALE = 8.0

        def shift_token(t):
            t1, t2 = jnp.split(t, 2, axis=-1)
            t2 = jnp.pad(t2, ((0, 0), (1, 0), (0, 0)))[:, :-1]
            return jnp.concatenate([t1, t2], axis=-1)

        def l2norm(t):
            return t / jnp.clip(jnp.linalg.norm(t, axis=-1, keepdims=True), 1e-12)

        def rotate_half(x):
            x1, x2 = jnp.split(x, 2, axis=-1)
            return jnp.concatenate([-x2, x1], axis=-1)

        def rotary_xpos(q, k):
            n = q.shape[-2]
            half_idx = jnp.arange(0, DIM_HEAD, 2, dtype=jnp.float32)
            inv_freq = 1.0 / 10000.0 ** (half_idx / DIM_HEAD)
            t = jnp.arange(n, dtype=jnp.float32)
            freqs = t[:, None] * inv_freq[None, :]
            freqs = jnp.concatenate([freqs, freqs], axis=-1)
            base = (half_idx + 0.4 * DIM_HEAD) / (1.4 * DIM_HEAD)
            power = (t - n // 2) / float(WINDOW // 2)
            scale = base[None, :] ** power[:, None]
            scale = jnp.concatenate([scale, scale], axis=-1)
            cos, sin = (jnp.cos(freqs), jnp.sin(freqs))
            q = q * cos * scale + rotate_half(q) * sin * scale
            k = k * cos / scale + rotate_half(k) * sin / scale
            return (q, k)

        def local_attention(q, k, v):
            b, h, n, d = q.shape
            w = n // WINDOW
            bq = q.reshape(b, h, w, WINDOW, d) * QK_SCALE
            bk = k.reshape(b, h, w, WINDOW, d)
            bv = v.reshape(b, h, w, WINDOW, d)

            def look_around(t):
                p = jnp.pad(t, ((0, 0), (0, 0), (1, 0), (0, 0), (0, 0)))
                return jnp.concatenate([p[:, :, :w], p[:, :, 1:]], axis=3)
            bk, bv = (look_around(bk), look_around(bv))
            bt = jnp.arange(n).reshape(w, WINDOW)
            btp = jnp.pad(bt, ((1, 0), (0, 0)), constant_values=-1)
            btk = jnp.concatenate([btp[:w], btp[1:]], axis=1)
            sim = jnp.einsum('bhwid,bhwjd->bhwij', bq, bk)
            i = bt[:, :, None]
            j = btk[:, None, :]
            mask = (i < j) | (i > j + WINDOW) | (j == -1)
            sim = jnp.where(mask, -jnp.finfo(sim.dtype).max, sim)
            attn = jax.nn.softmax(sim, axis=-1)
            out = jnp.einsum('bhwij,bhwjd->bhwid', attn, bv)
            return out.reshape(b, h, n, d)

        def _layer(x, wqkv, qs, ksc, wo, lg, lb, w1, b1, w2, b2):
            b, n, _ = x.shape
            h = shift_token(x)
            qkv = h @ wqkv
            q, k, v = jnp.split(qkv, 3, axis=-1)
            to_heads = lambda t: t.reshape(b, n, HEADS, DIM_HEAD).transpose(0, 2, 1, 3)
            q, k, v = (to_heads(q), to_heads(k), to_heads(v))
            q = l2norm(q) * qs
            k = l2norm(k) * ksc
            q, k = rotary_xpos(q, k)
            o = local_attention(q, k, v)
            o = o.transpose(0, 2, 1, 3).reshape(b, n, INNER)
            x = x + o @ wo
            h = shift_token(x)
            mu = h.mean(-1, keepdims=True)
            var = h.var(-1, keepdims=True)
            h = (h - mu) / jnp.sqrt(var + 1e-05) * lg + lb
            h = h @ w1 + b1
            a, g = jnp.split(h, 2, axis=-1)
            h = a * jax.nn.gelu(g, approximate=False)
            x = x + h @ w2 + b2
            return x
        for l in range(DEPTH):
            x = _layer(x, wqkv[l], q_scale[l], k_scale[l], wo[l], ln_g[l], ln_b[l], w1[l], b1[l], w2[l], b2[l])
        return x
    x = L0_attn_x
    x = x + _L0_attn_ref(_layernorm(x, axis=-1), L0_attn_delta, L0_attn_alpha, L0_attn_beta, L0_attn_gamma, L0_attn_omega)
    x = x + _L0_ffn_ref(_layernorm(x, axis=-1), L0_ffn_wqkv, L0_ffn_q_scale, L0_ffn_k_scale, L0_ffn_wo, L0_ffn_ln_g, L0_ffn_ln_b, L0_ffn_w1, L0_ffn_b1, L0_ffn_w2, L0_ffn_b2)
    return x

_drawn_inputs = setup_inputs


def setup_inputs(seed=0):
    import zlib

    import numpy as np

    out = dict(_drawn_inputs(seed))
    spreads = {'L0_ffn_q_scale': (1.0, 0.6),
     'L0_ffn_k_scale': (1.0, 0.6),
     'L0_ffn_ln_g': (1.0, 0.6),
     'L0_ffn_ln_b': (0.0, 0.8),
     'L0_ffn_b1': (0.0, 0.8),
     'L0_ffn_b2': (0.0, 0.8)}
    factors = {'L0_ffn_wqkv': 3.782, 'L0_ffn_wo': 3.756, 'L0_ffn_w1': 8.0, 'L0_ffn_w2': 8.0}
    for name, (base, spread) in spreads.items():
        noise = np.random.default_rng([zlib.crc32(name.encode()), seed]).standard_normal(out[name].shape)
        drawn = base * np.exp(spread * noise) if base else spread * noise
        out[name] = jnp.asarray(drawn.astype(out[name].dtype))
    for name, factor in factors.items():
        out[name] = (out[name] * factor).astype(out[name].dtype)
    return out
```

```python
from contextlib import ExitStack

import concourse.bass as bass
from concourse import mybir

F32 = mybir.dt.float32
BF16 = mybir.dt.bfloat16
ALU = mybir.AluOpType
ACT = mybir.ActivationFunctionType
AX = mybir.AxisListType

P = 128
SEQS, LEN, D = 16, 512, 128
BLKS = LEN // P
NBLK = SEQS * BLKS
STATES = 16
LAYERS, HEADS, DH, WINDOW = 2, 8, 64, 64
PAIRS = HEADS // 2
INNER = HEADS * DH
HID = int(D * 4 * 2 / 3)
HT = -(-HID // P)
EPS = 1e-5
NORM_MIN = 1e-12
QK_SCALE = 8.0
NEG = -1e30
VW = DH + 1

CH = 8
GROUPS = D // CH

LAG_LOAD = 0
LAG_PROJ = 1
LAG_QKT = 2
LAG_MAX = 3
LAG_SIM = 4
LAG_PV = 5
LAG_OT = 6
LAG_WO = 7
MLP_IN = 2
MLP_UP = 3
MLP_DOWN = 4
HEAD_ITERS = 4
TOTAL = LAYERS * NBLK
ITERS = TOTAL // BLKS + HEAD_ITERS

ROW_MAX = 64
ROW_FIRST = 96


def ema_part(nc, T):
    ctx = ExitStack()
    with ctx:
        def sb(name, shape, dt=F32):
            return ctx.enter_context(nc.sbuf_tensor(name, shape, dt))

        def sem(name):
            return ctx.enter_context(nc.semaphore(name))

        X = sb("X", [P, NBLK, D])
        Xr = sb("Xr", [P, NBLK, D])
        Y = T["xcur"][:, :, :].rearrange("p a b -> p (a b)").rearrange("p (d c) -> p d c", d=D)
        stats = sb("stats", [P, NBLK, 6])
        mv = sb("mv", [P, NBLK, 2])
        rstd = sb("rstd", [P, NBLK])
        nmr = sb("nmr", [P, NBLK])
        par_d = sb("par_d", [P, 4, STATES])
        om = sb("om", [P, 1])
        lnq_d = sb("lnq_d", [P, STATES])
        cf_d = sb("cf_d", [P, STATES])
        par_b = sb("par_b", [P, 2, D * STATES])
        dec = sb("dec", [P, D * STATES])
        par_n = sb("par_n", [STATES, 4, D])
        lnq_n = sb("lnq_n", [STATES, D])
        cf_n = sb("cf_n", [STATES, D])
        q128 = sb("q128", [STATES, D])
        ramps = sb("ramps", [P, 2 * P + 1])
        ramp = ramps[:, 0:P]
        ramp1 = ramps[:, P:2 * P]
        age = ramps[:, 2 * P:2 * P + 1]
        kpad = sb("kpad", [P, 2 * P])
        ktmp = sb("ktmp", [P, 2, P])
        toep = sb("toep", [P, 2, CH, P])
        cexp = sb("cexp", [STATES, 2, CH, P])
        S = sb("S", [STATES, 2, CH, NBLK])
        H = sb("H", [STATES, 2, CH, 3 * SEQS])
        pS = [ctx.enter_context(nc.psum_tensor(f"pS{i}", [P, 512], F32)) for i in range(2)]
        pO = [ctx.enter_context(nc.psum_tensor(f"pO{i}", [P, 512], F32)) for i in range(2)]

        xr_in = [sem(f"xr_in{i}") for i in range(4)]
        x_in = sem("x_in")
        par_in = sem("par_in")
        ramp_in = sem("ramp_in")
        stats_done = sem("stats_done")
        mv_done = sem("mv_done")
        ln_done = sem("ln_done")
        rstd_done = sem("rstd_done")
        y_done = sem("y_done")
        a_par = sem("a_par")
        v_par = sem("v_par")
        k_exp = sem("k_exp")
        k_acc = sem("k_acc")
        kpad_done = sem("kpad_done")
        k_zero = sem("k_zero")
        k_out = sem("k_out")
        toep_in = [sem(f"toep_in{i}") for i in range(2)]
        c_arg = sem("c_arg")
        c_done = sem("c_done")
        s_mm = sem("s_mm")
        h_step = sem("h_step")
        h_done = sem("h_done")
        o_mm = sem("o_mm")
        x1_add = sem("x1_add")
        x1_out = sem("x1_out")
        z_done = sem("z_done")

        x_d = T["x"].rearrange("a (b p) d -> p (a b) d", p=P)
        xr_d = T["x_rev"].rearrange("a (b p) d -> p (a b) d", p=P)
        x1_d = T["x1"].rearrange("a (b p) d -> p (a b) d", p=P)
        names = ("delta", "alpha", "beta", "gamma")
        block = ctx.enter_context(nc.Block())

        @block.sync
        def _(sp):
            for c in range(4):
                m = slice(c * 16, c * 16 + 16)
                sp.dma_start(Xr[:, m, :], xr_d[:, m, :]).then_inc(xr_in[c], 16)
            sp.dma_start(X[:, :, :], x_d).then_inc(x_in, 16)
            sp.wait_ge(kpad_done, 1)
            sp.dma_start(T["taps"], kpad[:, :]).then_inc(k_out, 16)
            sp.wait_ge(k_out, 16)
            for g in range(GROUPS):
                if g >= 2:
                    sp.wait_ge(o_mm, g - 1)
                sp.dma_start(toep[:, g % 2], bass.AP(tensor=T["taps"].tensor, offset=g * CH * 2 * P + 1,
                                                     ap=[[1, P], [2 * P, CH], [1, P]])).then_inc(toep_in[g % 2], 16)
            sp.wait_ge(x1_add, GROUPS)
            sp.dma_start(x1_d, X[:, :, :]).then_inc(x1_out, 16)
            sp.wait_ge(x1_out, 16)

        @block.scalar
        def _(act):
            for k, name in enumerate(names):
                flat = T[name].rearrange("d n -> (d n)")
                act.dma_start(par_d[:, k, :], T[name]).then_inc(par_in, 16)
                act.dma_start(par_n[:, k, :], T[name + "_t"]).then_inc(par_in, 16)
                if k < 2:
                    act.dma_start(par_b[:, k, :], bass.AP(tensor=flat.tensor, offset=0, ap=[[0, P], [1, D * STATES]])).then_inc(par_in, 16)
            act.dma_start(om[:, :], T["omega"].rearrange("(d a) -> d a", a=1)).then_inc(par_in, 16)
            act.dma_start(ramps[:, :], T["ramp"]).then_inc(ramp_in, 16)
            act.wait_ge(par_in, 16 * 11)
            nc.scalar.activation(par_d[:, 0:2, :], par_d[:, 0:2, :], ACT.Sigmoid).then_inc(a_par, 1)
            nc.scalar.activation(par_n[:, 0:2, :], par_n[:, 0:2, :], ACT.Sigmoid).then_inc(a_par, 1)
            nc.scalar.activation(par_b[:, :, :], par_b[:, :, :], ACT.Sigmoid).then_inc(a_par, 1)
            act.wait_ge(v_par, 3)
            nc.scalar.activation(lnq_d[:, :], lnq_d[:, :], ACT.Ln).then_inc(a_par, 1)
            nc.scalar.activation(lnq_n[:, :], lnq_n[:, :], ACT.Ln).then_inc(a_par, 1)
            nc.scalar.activation(dec[:, :], dec[:, :], ACT.Ln).then_inc(a_par, 1)
            act.wait_ge(a_par, 6)
            act.wait_ge(ramp_in, 16)
            for n in range(STATES):
                if n >= 2:
                    act.wait_ge(k_acc, n - 1)
                nc.scalar.activation(ktmp[:, n % 2, :], ramp[:, :], ACT.Exp, scale=lnq_d[:, n:n + 1]).then_inc(k_exp, 1)
            nc.scalar.activation(q128[:, :], lnq_n[:, :], ACT.Exp, scale=float(P)).then_inc(a_par, 1)
            nc.scalar.activation(dec[:, :], dec[:, :], ACT.Exp, scale=age[:, 0:1]).then_inc(a_par, 1)
            act.wait_ge(mv_done, NBLK + 1)
            nc.scalar.activation(rstd[:, :], rstd[:, :], ACT.Ln).then_inc(ln_done, 1)
            act.wait_ge(ln_done, 1)
            nc.scalar.activation(rstd[:, :], rstd[:, :], ACT.Exp, scale=-0.5).then_inc(rstd_done, 1)
            for g in range(GROUPS):
                act.wait_ge(c_arg, g + 1)
                nc.scalar.activation(cexp[:, g % 2], cexp[:, g % 2], ACT.Exp).then_inc(c_done, 1)
            act.wait_ge(mv_done, 2 * NBLK + 2)
            nc.scalar.activation(rstd[:, :], rstd[:, :], ACT.Ln).then_inc(ln_done, 1)
            act.wait_ge(ln_done, 2)
            nc.scalar.activation(rstd[:, :], rstd[:, :], ACT.Exp, scale=-0.5).then_inc(rstd_done, 1)

        @block.gpsimd
        def _(pool):
            pool.wait_ge(y_done, 1)
            for m in range(NBLK):
                col = (m % BLKS) * SEQS + m // BLKS
                nc.gpsimd.tensor_scalar(Y[:, :, col], Xr[:, m, :], rstd[:, m:m + 1], nmr[:, m:m + 1],
                                        ALU.mult, ALU.add).then_inc(y_done, 1)

        @block.vector
        def _(dve):
            nc.vector.memset(kpad[:, :], 0.0).then_inc(k_zero, 1)
            dve.wait_ge(k_zero, 1)
            dve.wait_ge(a_par, 3)
            for k, (q, a, b) in enumerate(((lnq_d[:, :], par_d[:, 0, :], par_d[:, 1, :]),
                                           (lnq_n[:, :], par_n[:, 0, :], par_n[:, 1, :]),
                                           (dec[:, :], par_b[:, 0, :], par_b[:, 1, :]))):
                nc.vector.tensor_tensor(q, a, b, ALU.mult).then_inc(stats_done, 1)
                dve.wait_ge(stats_done, k + 1)
                nc.vector.tensor_scalar(q, q, -1.0, 1.0, ALU.mult, ALU.add).then_inc(v_par, 1)
            for k, (c, par) in enumerate(((cf_d[:, :], par_d), (cf_n[:, :], par_n))):
                nc.vector.tensor_tensor(c, par[:, 0, :], par[:, 2, :], ALU.mult).then_inc(stats_done, 1)
                dve.wait_ge(stats_done, 4 + 2 * k)
                nc.vector.scalar_tensor_tensor(c, c, float(STATES) ** -0.5, par[:, 3, :],
                                               ALU.mult, ALU.mult).then_inc(stats_done, 1)
                dve.wait_ge(stats_done, 5 + 2 * k)
            for n in range(STATES):
                dve.wait_ge(k_exp, n + 1)
                if n:
                    dve.wait_ge(k_acc, n)
                nc.vector.scalar_tensor_tensor(kpad[:, P:2 * P], ktmp[:, n % 2, :], cf_d[:, n:n + 1],
                                               kpad[:, P:2 * P], ALU.mult, ALU.add).then_inc(k_acc, 1)
            dve.wait_ge(k_acc, STATES)
            nc.vector.tensor_tensor(kpad[:, P:P + 1], kpad[:, P:P + 1], om[:, :], ALU.add).then_inc(kpad_done, 1)

            def layer_norm_stats(round_):
                done = 7 + round_ * NBLK
                tokens = X if round_ else Xr
                for m in range(NBLK):
                    if round_ == 0 and m % 16 == 0:
                        dve.wait_ge(xr_in[m // 16], 16)
                    nc.vector.bn_stats(stats[:, m, :], tokens[:, m, :]).then_inc(stats_done, 1)
                    if m:
                        dve.wait_ge(stats_done, done + m)
                        nc.vector.bn_aggr(mv[:, m - 1, :], stats[:, m - 1, :]).then_inc(mv_done, 1)
                dve.wait_ge(stats_done, done + NBLK)
                nc.vector.bn_aggr(mv[:, NBLK - 1, :], stats[:, NBLK - 1, :]).then_inc(mv_done, 1)
                dve.wait_ge(mv_done, NBLK + round_ * (NBLK + 1))
                nc.vector.tensor_scalar(rstd[:, :], mv[:, :, 1], EPS, None, ALU.add).then_inc(mv_done, 1)
                dve.wait_ge(rstd_done, round_ + 1)
                nc.vector.scalar_tensor_tensor(nmr[:, :], mv[:, :, 0], -1.0, rstd[:, :],
                                               ALU.mult, ALU.mult).then_inc(y_done if round_ == 0 else z_done, 1)

            layer_norm_stats(0)

            def state_arguments(g):
                if g >= 2:
                    dve.wait_ge(o_mm, g - 1)
                nc.vector.tensor_tensor(
                    cexp[:, g % 2], lnq_n[:, g * CH:g * CH + CH].unsqueeze(2).broadcast_to([STATES, CH, P]),
                    ramp1[0:STATES, :].unsqueeze(1).broadcast_to([STATES, CH, P]), ALU.mult).then_inc(c_arg, 1)

            def carry_states(g):
                if g >= 2:
                    dve.wait_ge(o_mm, g - 1)
                dve.wait_ge(s_mm, g + 1)
                s = S[:, g % 2]
                h = H[:, g % 2]
                cf = cf_n[:, g * CH:g * CH + CH].unsqueeze(2).broadcast_to([STATES, CH, NBLK])
                qq = q128[:, g * CH:g * CH + CH].unsqueeze(2).broadcast_to([STATES, CH, SEQS])
                nc.vector.tensor_tensor(s, pS[g % 2][0:STATES, :].rearrange("p (c m) -> p c m", c=CH), cf,
                                        ALU.mult).then_inc(h_step, 1)
                dve.wait_ge(h_step, 6 * g + 1)
                nc.vector.tensor_copy(h[:, :, 0:SEQS], s[:, :, 0:SEQS]).then_inc(h_step, 1)
                for j in (1, 2):
                    dve.wait_ge(h_step, 6 * g + 2 * j)
                    nc.vector.tensor_tensor(h[:, :, j * SEQS:(j + 1) * SEQS], h[:, :, (j - 1) * SEQS:j * SEQS], qq,
                                            ALU.mult).then_inc(h_step, 1)
                    dve.wait_ge(h_step, 6 * g + 2 * j + 1)
                    nc.vector.tensor_tensor(h[:, :, j * SEQS:(j + 1) * SEQS], h[:, :, j * SEQS:(j + 1) * SEQS],
                                            s[:, :, j * SEQS:(j + 1) * SEQS], ALU.add).then_inc(h_step, 1)
                dve.wait_ge(h_step, 6 * g + 6)

            def add_out(g):
                dve.wait_ge(o_mm, g + 1)
                xv = X[:, :, g * CH:(g + 1) * CH].rearrange("p (s b) d -> p d b s", b=BLKS)
                ov = pO[g % 2][:, :].rearrange("p (d b s) -> p d b s", d=CH, b=BLKS)
                for b in range(BLKS):
                    last = nc.vector.tensor_tensor(xv[:, :, b], xv[:, :, b], ov[:, :, b], ALU.add)
                last.then_inc(x1_add, 1)

            dve.wait_ge(a_par, 8)
            for g in range(GROUPS + 2):
                if g < GROUPS:
                    state_arguments(g)
                if 1 <= g <= GROUPS:
                    carry_states(g - 1)
                    nc.vector.tensor_copy(ktmp[0:1, 0, 0:1], ktmp[0:1, 1, 0:1]).then_inc(h_done, 1)
                if g >= 2:
                    if g == 2:
                        dve.wait_ge(x_in, 16)
                    add_out(g - 2)
            dve.wait_ge(x1_add, GROUPS)
            layer_norm_stats(1)
            dve.wait_ge(z_done, 1)
            for m in range(NBLK):
                nc.vector.tensor_scalar(T["xcur"][:, m, :], X[:, m, :], rstd[:, m:m + 1], nmr[:, m:m + 1],
                                        ALU.mult, ALU.add).then_inc(z_done, 1)
            dve.wait_ge(z_done, NBLK + 1)

        @block.tensor
        def _(pe):
            decays = dec[:, :].rearrange("p (d n) -> p d n", d=D)
            pe.wait_ge(a_par, 8)
            pe.wait_ge(y_done, NBLK + 1)

            def states(g):
                if g >= 2:
                    pe.wait_ge(h_step, 6 * (g - 2) + 1)
                for c in range(CH):
                    last = nc.tensor.matmul(pS[g % 2][0:STATES, c * NBLK:(c + 1) * NBLK], decays[:, g * CH + c, :],
                                            Y[:, g * CH + c, :], start=True, stop=True)
                last.then_inc(s_mm, 1)

            def outputs(g):
                pe.wait_ge(toep_in[g % 2], 16 * (g // 2 + 1))
                if g >= 2:
                    pe.wait_ge(x1_add, g - 1)
                for c in range(CH):
                    last = nc.tensor.matmul(pO[g % 2][:, c * NBLK:(c + 1) * NBLK], toep[:, g % 2, c, :],
                                            Y[:, g * CH + c, :], start=(c == 0), stop=False, skip_group_check=True)
                pe.wait_ge(c_done, g + 1)
                pe.wait_ge(h_done, g + 1)
                for c in range(CH):
                    last = nc.tensor.matmul(pO[g % 2][:, c * NBLK + SEQS:(c + 1) * NBLK], cexp[:, g % 2, c, :],
                                            H[:, g % 2, c, :], start=False, stop=(c == CH - 1), skip_group_check=True)
                last.then_inc(o_mm, 1)

            states(0)
            for g in range(GROUPS):
                if g + 1 < GROUPS:
                    states(g + 1)
                outputs(g)


def stack_part(nc, T):
    ctx = ExitStack()
    with ctx:
        def sb(name, shape, dt=F32):
            return ctx.enter_context(nc.sbuf_tensor(name, shape, dt))

        def sem(name):
            return ctx.enter_context(nc.semaphore(name))

        x = T["xcur"]
        wqkv = sb("wqkv", [P, LAYERS, 3 * INNER])
        wo = sb("wo", [P, LAYERS, PAIRS, D])
        w1 = sb("w1", [P, LAYERS, 2 * HID])
        w2 = sb("w2", [P, LAYERS, HT, D])
        b1 = sb("b1", [P, LAYERS, 2, HT])
        b2 = sb("b2", [P, LAYERS, D])
        lg = sb("lg", [P, LAYERS])
        lb = sb("lb", [P, LAYERS])
        rope = sb("rope", [P, BLKS, 4 * DH])
        scl = sb("scl", [P, LAYERS, 4 * DH])
        tab = sb("tab", [P, LAYERS, BLKS, 4 * DH])
        ident = sb("ident", [P, P])
        halves = sb("halves", [P, 2])
        identb = sb("identb", [P, P], BF16)
        mask_n = sb("mask_n", [P, 2, P], BF16)
        mask_t = sb("mask_t", [P, HEADS, P], BF16)

        xs = sb("xs", [P, BLKS, D])
        hT = sb("hT", [P, 2, P])
        u = sb("u", [P, 2, 2 * INNER])
        sq = sb("sq", [P, 2 * INNER])
        ss = sb("ss", [P, 2, 2 * HEADS])
        rn = sb("rn", [P, 2, 2 * HEADS])
        minus_half = sb("minus_half", [P, 2 * HEADS])
        t1 = sb("t1", [P, 2 * INNER])
        t2 = sb("t2", [P, 2 * INNER])
        qk = sb("qk", [P, 2 * INNER])
        qz = sb("qz", [P, BLKS, PAIRS, 2, P])
        kT = sb("kT", [P, PAIRS, WINDOW + LEN])
        qb = sb("qb", [P, BLKS, PAIRS, P], BF16)
        kzb = sb("kzb", [P, PAIRS, 2, WINDOW + LEN], BF16)
        nmax = sb("nmax", [P, HEADS])
        nm2 = sb("nm2", [P, 2, 2 * HEADS], BF16)
        R = sb("R", [P, BLKS, P], BF16)
        pT = sb("pT", [P, 2, HEADS, P])
        V = sb("V", [P, BLKS, HEADS, VW])
        Vs = sb("Vs", [P, BLKS, HEADS, VW])
        rden = sb("rden", [P, 2, PAIRS])
        O = sb("O", [P, 2, INNER])
        OT = sb("OT", [P, 2, PAIRS, P])
        ms = sb("ms", [P, BLKS, D])
        mst = sb("mst", [P, BLKS, 6])
        mmv = sb("mmv", [P, BLKS, 2])
        mrs = sb("mrs", [P, BLKS])
        mnm = sb("mnm", [P, BLKS])
        mln = sb("mln", [P, BLKS, D])
        h2T = sb("h2T", [P, LEN])
        ha = sb("ha", [P, HT, LEN])
        hg = sb("hg", [P, HT, LEN])
        x1 = sb("x1", [P, BLKS, D])

        def bank(name, n=1):
            return ctx.enter_context(nc.psum_tensor(name, [P, 512 * n], F32))

        p_qk = bank("p_qk", 2)
        p_v = bank("p_v")
        p_small = bank("p_small")
        p_max = bank("p_max", 2)
        p_sim = bank("p_sim", 2)

        w_in = sem("w_in")
        tab_done = sem("tab_done")
        init_done = sem("init_done")
        xs_in = [sem(f"xs_in{b}") for b in range(BLKS)]
        vs_in = [sem(f"vs_in{b}") for b in range(BLKS)]
        ms_in = sem("ms_in")
        x1_in = sem("x1_in")
        out_done = sem("out_done")
        mt_mm = sem("mt_mm")
        mt_copied = sem("mt_copied")
        qk_mm = sem("qk_mm")
        u_copied = sem("u_copied")
        squared = sem("squared")
        ss_done = sem("ss_done")
        clamped = sem("clamped")
        rn_done = sem("rn_done")
        cos_done = sem("cos_done")
        sin_done = sem("sin_done")
        rot_done = sem("rot_done")
        qk_done = sem("qk_done")
        qkt_mm = sem("qkt_mm")
        qkt_copied = sem("qkt_copied")
        bf_done = sem("bf_done")
        max_mm = sem("max_mm")
        max_done = sem("max_done")
        nm_hi = sem("nm_hi")
        nm_done = sem("nm_done")
        sim_mm = sem("sim_mm")
        exp_done = sem("exp_done")
        ht_mm = sem("ht_mm")
        ht_copied = sem("ht_copied")
        pv_mm = sem("pv_mm")
        rden_done = sem("rden_done")
        o_done = sem("o_done")
        v_mm = sem("v_mm")
        v_copied = sem("v_copied")
        ot_mm = sem("ot_mm")
        ot_copied = sem("ot_copied")
        wo_mm = sem("wo_mm")
        wo_added = sem("wo_added")
        m_stats = sem("m_stats")
        m_var = sem("m_var")
        m_rstd = sem("m_rstd")
        m_nmr = sem("m_nmr")
        m_norm = sem("m_norm")
        b2_added = sem("b2_added")
        m_tr = sem("m_tr")
        m_trc = sem("m_trc")
        up_mm = sem("up_mm")
        g_copied = sem("g_copied")
        a_copied = sem("a_copied")
        gelu_done = sem("gelu_done")
        hid_done = sem("hid_done")
        down_mm = sem("down_mm")
        mlp_added = sem("mlp_added")
        fin_done = sem("fin_done")
        held = sem("held")

        def iterate(eng, body):
            per_layer = SEQS
            for i in range(HEAD_ITERS):
                body(i, None)
            with eng.Fori(HEAD_ITERS, per_layer) as i:
                body(i, 0)
            for i in range(per_layer, per_layer + HEAD_ITERS):
                body(i, None)
            with eng.Fori(per_layer + HEAD_ITERS, 2 * per_layer) as i:
                body(i, 1)
            for i in range(2 * per_layer, ITERS):
                body(i, None)

        def block_at(i, b, lag, layer):
            m = i * BLKS + (b - lag)
            q = i + (b - lag) // BLKS
            if layer is None:
                return (m, m % BLKS, m // NBLK, q) if 0 <= m < TOTAL else None
            return m, (b - lag) % BLKS, layer, q

        def seq_at(i, lag, layer):
            s = i - lag
            if layer is None:
                return (s, s // SEQS) if 0 <= s < TOTAL // BLKS else None
            return s, layer

        def need(eng, semaphore, count):
            if not isinstance(count, int) or count > 0:
                eng.wait_ge(semaphore, count)

        def hold(eng, semaphore, count):
            need(eng, semaphore, count)
            if not isinstance(count, int):
                eng.sem_inc(held, 1)

        def capped(count):
            return min(count, TOTAL) if isinstance(count, int) else count

        def row_of(m, layer):
            return m - layer * NBLK

        block = ctx.enter_context(nc.Block())

        @block.sync
        def _(sp):
            w_h = [(wqkv[:, :, :], T["wqkv"].rearrange("l p n -> p l n")),
                   (ident[:, :], T["ident"]),
                   (identb[:, :], T["identb"]),
                   (halves[:, :], T["halves"]),
                   (mask_n[:, :, :], T["mask_n"]),
                   (mask_t[:, :, :], T["mask_t"]),
                   (rope[:, :, :], T["rope"]),
                   (wo[:, :, :, :], T["wo"].rearrange("l (k p) n -> p l k n", p=P)),
                   (w1[:, :, :], T["w1"].rearrange("l p n -> p l n")),
                   (b1[:, :, :, :], T["b1_t"]),
                   (lg[:, :], T["ln_g_t"]),
                   (lb[:, :], T["ln_b_t"]),
                   (b2[:, :, :], bass.AP(tensor=T["b2"].tensor, offset=0, ap=[[0, P], [D, LAYERS], [1, D]]))]
            half = DH // 2
            for k, name in enumerate(("q_scale", "k_scale")):
                def piece(at, frm, n):
                    return (scl[:, :, at:at + n], bass.AP(tensor=T[name].tensor, offset=frm, ap=[[0, P], [DH, LAYERS], [1, n]]))
                w_h += [piece(k * DH, 0, DH), piece((2 + k) * DH, half, half), piece((2 + k) * DH + half, 0, half)]
            for l in range(LAYERS):
                for t in range(HT):
                    rows = min(P, HID - t * P)
                    w_h.append((w2[0:rows, l, t, :], T["w2"][l, t * P:t * P + rows, :]))
            assert len(w_h) == N_WEIGHT_DMAS
            for dst, src in w_h:
                sp.dma_start(dst, src).then_inc(w_in, 16)
            sp.wait_ge(init_done, N_INIT)

            def shift_in(m, b, l, q):
                hold(sp, ht_mm, m - 3)
                if l:
                    hold(sp, mlp_added, q - SEQS + 1)
                r = row_of(m, l)
                sp.dma_start(xs[:, b, 0:DH], x[:, r, 0:DH]).then_inc(xs_in[b], 16)
                sp.dma_start(xs[1:P, b, DH:D], x[0:P - 1, r, DH:D]).then_inc(xs_in[b], 16)
                if b:
                    sp.dma_start(xs[0:1, b, DH:D], x[P - 1:P, r - 1, DH:D]).then_inc(xs_in[b], 16)

            def shift_v(m, b, l, q):
                hold(sp, v_copied, m + 1)
                hold(sp, pv_mm, m - 3)
                sp.dma_start(Vs[DH:P, b, :, :], V[0:DH, b, :, :]).then_inc(vs_in[b], 16)
                if b:
                    sp.dma_start(Vs[0:DH, b, :, :], V[DH:P, b - 1, :, :]).then_inc(vs_in[b], 16)

            def mlp_in(s, l):
                hold(sp, wo_added, (s + 1) * BLKS)
                hold(sp, m_norm, s)
                r = (s - l * SEQS) * BLKS
                sp.dma_start(ms[:, :, 0:DH], x[:, bass.ds(r, BLKS), 0:DH]).then_inc(ms_in, 16)
                sp.dma_start(ms[1:P, :, DH:D], x[0:P - 1, bass.ds(r, BLKS), DH:D]).then_inc(ms_in, 16)
                sp.dma_start(ms[0:1, 1:BLKS, DH:D], x[P - 1:P, bass.ds(r, BLKS - 1), DH:D]).then_inc(ms_in, 16)

            def final(s, l):
                q = s - l * SEQS
                hold(sp, fin_done, q + 1)
                sp.dma_start(out_d[:, bass.ds(q * BLKS, BLKS), :], x[:, bass.ds(q * BLKS, BLKS), :]).then_inc(out_done, 16)

            def load_x1(s, l):
                q = s - l * SEQS
                hold(sp, fin_done, q)
                sp.dma_start(x1[:, :, :], x1_d[:, bass.ds(q * BLKS, BLKS), :]).then_inc(x1_in, 16)

            def body(i, layer):
                for b in range(BLKS):
                    at = block_at(i, b, LAG_LOAD, layer)
                    if at:
                        shift_in(*at)
                    at = block_at(i, b, LAG_PROJ + 1, layer)
                    if at:
                        shift_v(*at)
                    if b == 1:
                        at = seq_at(i, MLP_DOWN, layer)
                        if at and at[1] == LAYERS - 1:
                            final(*at)
                        at = seq_at(i, MLP_UP, layer)
                        if at and at[1] == LAYERS - 1:
                            load_x1(*at)
                    if b == BLKS - 1:
                        at = seq_at(i, MLP_IN, layer)
                        if at:
                            mlp_in(*at)

            x1_d = T["x1"].rearrange("a (b p) d -> p (a b) d", p=P)
            out_d = T["out"].rearrange("a (b p) d -> p (a b) d", p=P)
            iterate(sp, body)
            sp.wait_ge(out_done, 16 * SEQS)

        @block.tensor
        def _(pe):
            pe.wait_ge(w_in, 16 * N_WEIGHT_DMAS)
            pe.wait_ge(init_done, N_INIT)

            def transpose_maxima(m, b, l, q):
                need(pe, nm_done, m + 1)
                need(pe, wo_added, m - (LAG_WO - LAG_SIM))
                need(pe, ht_copied, capped(m + (LAG_SIM - LAG_LOAD)))
                nc.tensor.transpose(p_small[0:2 * HEADS, 0:DH].bitcast(BF16), nm2[:, b % 2], identb[:, :]).then_inc(mt_mm, 1)

            def project_qk(m, b, l, q):
                need(pe, ht_copied, m + 1)
                need(pe, o_done, m - (LAG_PV - LAG_PROJ))
                need(pe, u_copied, m)
                for j in range(2):
                    last = nc.tensor.matmul(p_qk[:, j * 512:(j + 1) * 512], hT[:, b % 2, :],
                                            wqkv[:, l, j * INNER:(j + 1) * INNER], start=True, stop=True)
                last.then_inc(qk_mm, 1)

            def score_maxima(m, b, l, q):
                need(pe, bf_done, m + 1)
                need(pe, qkt_copied, capped(m + (LAG_MAX - LAG_QKT)))
                need(pe, max_done, m)
                for j in range(2):
                    nc.tensor.matmul(p_max[:, j * 512:(j + 1) * 512], identb[:, :],
                                     mask_n[:, 1 if b == 0 else 0, :].unsqueeze(1).broadcast_to([P, 4, P]),
                                     start=True, stop=False, skip_group_check=True)
                for v in range(2):
                    for p in range(PAIRS):
                        key = (2 * b + v) * WINDOW
                        last = nc.tensor.matmul(p_max[v * 64:v * 64 + 64, p * 256:(p + 1) * 256],
                                                qb[:, b, p, v * WINDOW:(v + 1) * WINDOW],
                                                kzb[:, p, :, key:key + 2 * WINDOW],
                                                start=False, stop=True, skip_group_check=True)
                last.then_inc(max_mm, 1)

            def score(m, b, l, q):
                need(pe, mt_copied, m + 1)
                need(pe, exp_done, m)
                for h in range(HEADS):
                    nc.tensor.matmul(p_sim[:, h * P:(h + 1) * P], mask_t[:, h, :], R[:, b, :],
                                     start=(h % 4 == 0), stop=False, skip_group_check=True)
                heads = p_sim[:, :].rearrange("p (h q) -> p h q", h=HEADS)
                for p in range(PAIRS):
                    for v in range(2):
                        key = (2 * b + v) * WINDOW
                        cols = slice(v * WINDOW, (v + 1) * WINDOW)
                        last = nc.tensor.matmul(heads[:, 2 * p:2 * p + 2, cols], kT[:, p, key:key + 2 * WINDOW],
                                                qz[:, b, p, :, cols], start=False, stop=True, skip_group_check=True)
                last.then_inc(sim_mm, 1)

            def transpose_input(m, b, l, q):
                need(pe, xs_in[b], 16 * (3 if b else 2) * (q + 1))
                need(pe, mt_copied, m - (LAG_SIM - LAG_LOAD) + 1)
                need(pe, ht_copied, m)
                nc.tensor.transpose(p_small[:, 0:P], xs[:, b, :], ident[:, :]).then_inc(ht_mm, 1)

            def values(m, b, l, q):
                need(pe, u_copied, capped(m + (LAG_PV - LAG_PROJ) + 1))
                need(pe, o_done, m)
                need(pe, exp_done, m + 1)
                need(pe, vs_in[b], 16 * (2 if b else 1) * (q + 1))
                for v, vals in ((0, Vs), (1, V)):
                    for h in range(HEADS):
                        at = (h // 4) * 512 + (h % 4) * VW
                        last = nc.tensor.matmul(p_qk[v * 64:v * 64 + 64, at:at + VW],
                                                pT[:, b % 2, h, v * WINDOW:(v + 1) * WINDOW],
                                                vals[:, b, h, :], start=True, stop=True)
                last.then_inc(pv_mm, 1)

            def project_v(m, b, l, q):
                need(pe, ot_copied, m - (LAG_OT - LAG_PROJ))
                need(pe, v_copied, m)
                nc.tensor.matmul(p_v[:, :], hT[:, b % 2, :], wqkv[:, l, 2 * INNER:3 * INNER],
                                 start=True, stop=True).then_inc(v_mm, 1)

            def transpose_qk(m, b, l, q):
                need(pe, qk_done, m + 1)
                need(pe, max_done, m - (LAG_MAX - LAG_QKT) + 1)
                need(pe, qkt_copied, m)
                for t in range(2 * PAIRS):
                    last = nc.tensor.transpose(p_max[:, t * P:(t + 1) * P], qk[:, t * P:(t + 1) * P], ident[:, :])
                last.then_inc(qkt_mm, 1)

            def project_out(m, b, l, q):
                need(pe, ot_copied, m + 1)
                need(pe, mt_copied, capped(m + (LAG_WO - LAG_SIM) + 1))
                need(pe, ht_copied, capped(m + (LAG_WO - LAG_LOAD) + 1))
                need(pe, wo_added, m)
                for p in range(PAIRS):
                    last = nc.tensor.matmul(p_small[:, 0:D], OT[:, b % 2, p, :], wo[:, l, p, :],
                                            start=(p == 0), stop=(p == PAIRS - 1))
                last.then_inc(wo_mm, 1)

            def transpose_out(m, b, l, q):
                need(pe, o_done, m + 1)
                need(pe, v_copied, capped(m + (LAG_OT - LAG_PROJ) + 1))
                need(pe, ot_copied, m)
                for p in range(PAIRS):
                    last = nc.tensor.transpose(p_v[:, p * P:(p + 1) * P], O[:, b % 2, p * P:(p + 1) * P], ident[:, :])
                last.then_inc(ot_mm, 1)

            def mlp_down(s, l):
                need(pe, hid_done, s + 1)
                for b in range(BLKS):
                    for t in range(HT):
                        rows = min(P, HID - t * P)
                        last = nc.tensor.matmul(p_sim[:, 512 + b * D:512 + (b + 1) * D],
                                                ha[0:rows, t, b * P:(b + 1) * P], w2[0:rows, l, t, :],
                                                start=(t == 0), stop=(t == HT - 1))
                last.then_inc(down_mm, 1)

            def mlp_transpose(s, l):
                need(pe, m_norm, s + 1)
                for b in range(BLKS):
                    last = nc.tensor.transpose(p_sim[:, b * P:(b + 1) * P], mln[:, b, :], ident[:, :])
                last.then_inc(m_tr, 1)

            def mlp_up(s, l, t):
                need(pe, m_trc, s + 1)
                rows = min(P, HID - t * P)
                for g in range(2):
                    last = nc.tensor.matmul(p_sim[0:rows, g * 512:(g + 1) * 512],
                                            w1[:, l, g * HID + t * P:g * HID + t * P + rows], h2T[:, :],
                                            start=True, stop=True)
                last.then_inc(up_mm, 1)

            def mlp_has_left(i, b, layer):
                if b == 0:
                    i, b = i - 1, BLKS
                up = seq_at(i, MLP_UP, layer)
                down = seq_at(i, MLP_DOWN, layer)
                if b == 1:
                    if down:
                        need(pe, mlp_added, down[0] + 1)
                    if up:
                        need(pe, m_trc, up[0] + 1)
                elif up:
                    need(pe, g_copied, up[0] * HT + b - 1)
                    need(pe, a_copied, up[0] * HT + b - 1)

            def body(i, layer):
                up = seq_at(i, MLP_UP, layer)
                down = seq_at(i, MLP_DOWN, layer)
                for b in range(BLKS):
                    def do(step, lag):
                        at = block_at(i, b, lag, layer)
                        if at:
                            step(*at)
                        return at

                    do(transpose_maxima, LAG_SIM)
                    do(project_qk, LAG_PROJ)
                    do(score_maxima, LAG_MAX)
                    mlp_has_left(i, b, layer)
                    sim = do(score, LAG_SIM)
                    do(transpose_input, LAG_LOAD)
                    do(values, LAG_PV)
                    do(project_v, LAG_PROJ)
                    do(transpose_qk, LAG_QKT)
                    do(project_out, LAG_WO)
                    if sim and (up or down):
                        need(pe, exp_done, sim[0] + 1)
                    if b == 0:
                        if down:
                            mlp_down(*down)
                        if up:
                            mlp_transpose(*up)
                    elif up:
                        mlp_up(*up, b - 1)
                    do(transpose_out, LAG_OT)

            iterate(pe, body)

        @block.scalar
        def _(act):
            act.wait_ge(w_in, 16 * N_WEIGHT_DMAS)
            act.wait_ge(init_done, N_INIT)

            def copy_input(m, b, l, q):
                need(act, ht_mm, m + 1)
                need(act, v_mm, m - 1)
                nc.scalar.activation(hT[:, b % 2, :], p_small[:, 0:P], ACT.Copy).then_inc(ht_copied, 1)

            def copy_qk(m, b, l, q):
                need(act, qk_mm, m + 1)
                need(act, cos_done, m - 1)
                need(act, sin_done, m - 1)
                need(act, squared, m - 1)
                nc.scalar.activation(u[:, b % 2, :], p_qk[:, :], ACT.Copy).then_inc(u_copied, 1)

            def square(m, b, l, q):
                need(act, u_copied, m + 1)
                need(act, ss_done, m)
                nc.scalar.activation(sq[:, :], u[:, b % 2, :], ACT.Square).then_inc(squared, 1)

            def softmax_exp(m, b, l, q):
                need(act, sim_mm, m + 1)
                need(act, pv_mm, m - 1)
                nc.scalar.activation(pT[:, b % 2], p_sim[:, :].rearrange("p (h q) -> p h q", h=HEADS), ACT.Exp).then_inc(exp_done, 1)

            def copy_v(m, b, l, q):
                need(act, v_mm, m + 1)
                need(act, pv_mm, m - 3)
                need(act, vs_in[(b - 3) % BLKS], 16 * (2 if (b - 3) % BLKS else 1) * (q + (b - 3) // BLKS + 1))
                nc.scalar.activation(V[:, b, :, 0:DH], p_v[:, :].rearrange("p (h d) -> p h d", h=HEADS), ACT.Copy).then_inc(v_copied, 1)

            def copy_qkt(m, b, l, q):
                need(act, qkt_mm, m + 1)
                need(act, sim_mm, m - 3)
                ps = p_max[:, :].rearrange("p (c t) -> p c t", c=2 * PAIRS)
                for h in range(2):
                    half = slice(h * DH, (h + 1) * DH)
                    nc.scalar.activation(qz[half, b, :, h, :], ps[half, 0:PAIRS, :], ACT.Copy)
                nc.scalar.activation(kT[:, :, WINDOW + b * P:WINDOW + (b + 1) * P], ps[:, PAIRS:2 * PAIRS, :],
                                     ACT.Copy).then_inc(qkt_copied, 1)

            def copy_out(m, b, l, q):
                need(act, ot_mm, m + 1)
                need(act, wo_mm, m - 1)
                nc.scalar.activation(OT[:, b % 2], p_v[:, :].rearrange("p (c t) -> p c t", c=PAIRS), ACT.Copy).then_inc(ot_copied, 1)

            def mlp_copy_input(s, l):
                need(act, m_tr, s + 1)
                need(act, up_mm, s * HT)
                nc.scalar.activation(h2T[:, :], p_sim[:, 0:512], ACT.Identity, bias=lb[:, l:l + 1],
                                     scale=lg[:, l:l + 1]).then_inc(m_trc, 1)

            def mlp_gate(s, l, t):
                rows = min(P, HID - t * P)
                need(act, up_mm, s * HT + t + 1)
                need(act, hid_done, s)
                nc.scalar.activation(hg[0:rows, t, :], p_sim[0:rows, 512:1024], ACT.Identity,
                                     bias=b1[0:rows, l, 1, t:t + 1]).then_inc(g_copied, 1)

            def mlp_gelu(s, l):
                need(act, g_copied, (s + 1) * HT)
                nc.scalar.activation(hg[:, :, :], hg[:, :, :], ACT.Gelu).then_inc(gelu_done, 1)

            def body(i, layer):
                up = seq_at(i, MLP_UP, layer)
                for b in range(BLKS):
                    def do(step, lag):
                        at = block_at(i, b, lag, layer)
                        if at:
                            step(*at)

                    do(copy_qk, LAG_PROJ)
                    do(square, LAG_PROJ)
                    do(softmax_exp, LAG_SIM)
                    do(copy_input, LAG_LOAD)
                    do(copy_v, LAG_PROJ)
                    do(copy_qkt, LAG_QKT)
                    if b == 0 and up:
                        mlp_copy_input(*up)
                    if b and up:
                        mlp_gate(*up, b - 1)
                    do(copy_out, LAG_OT)
                    if b == BLKS - 1 and up:
                        mlp_gelu(*up)

            iterate(act, body)

        @block.vector
        def _(dve):
            dve.wait_ge(w_in, 16 * N_WEIGHT_DMAS)
            for l in range(LAYERS):
                nc.vector.tensor_tensor(tab[:, l], rope[:, :, :],
                                        scl[:, l, :].unsqueeze(1).broadcast_to([P, BLKS, 4 * DH]), ALU.mult).then_inc(tab_done, 1)
            dve.wait_ge(tab_done, LAYERS)

            def table(l, b, part):
                t = tab[:, l, b, part * 2 * DH:(part + 1) * 2 * DH].rearrange("p (k d) -> p k d", k=2)
                return t.unsqueeze(2).broadcast_to([P, 2, HEADS, DH])

            def copy_maxima(m, b, l, q):
                need(dve, mt_mm, m + 1)
                need(dve, sim_mm, m - 3)
                nc.vector.tensor_copy(R[ROW_MAX:ROW_MAX + 2 * HEADS, b, :], p_small[0:2 * HEADS, 0:DH].bitcast(BF16)).then_inc(mt_copied, 1)

            def cosine(m, b, l, q):
                need(dve, u_copied, m + 1)
                need(dve, qk_done, m)
                nc.vector.tensor_tensor(t1[:, :].rearrange("p (k h d) -> p k h d", k=2, h=HEADS),
                                        u[:, b % 2, :].rearrange("p (k h d) -> p k h d", k=2, h=HEADS),
                                        table(l, b, 0), ALU.mult).then_inc(cos_done, 1)

            def sum_squares(m, b, l, q):
                need(dve, squared, m + 1)
                need(dve, rn_done, m - 1)
                nc.vector.tensor_reduce(ss[:, b % 2, :], sq[:, :].rearrange("p (h d) -> p h d", d=DH), AX.X, ALU.add).then_inc(ss_done, 1)
                need(dve, ss_done, m + 1)
                nc.vector.tensor_scalar(ss[:, b % 2, :], ss[:, b % 2, :], NORM_MIN ** 2, None, ALU.max).then_inc(clamped, 1)

            def maxima(m, b, l, q):
                need(dve, max_mm, m + 1)
                need(dve, nm_done, m)
                nc.vector.tensor_reduce(nmax[:, :], p_max[:, :].rearrange("p (h j) -> p h j", h=HEADS), AX.X,
                                        ALU.max, negate=True).then_inc(max_done, 1)
                need(dve, max_done, m + 1)
                need(dve, mt_mm, m - 1)
                nc.vector.tensor_copy(nm2[:, b % 2, 0:HEADS], nmax[:, :]).then_inc(nm_hi, 1)
                need(dve, nm_hi, m + 1)
                nc.vector.tensor_tensor(nm2[:, b % 2, HEADS:2 * HEADS], nmax[:, :], nm2[:, b % 2, 0:HEADS],
                                        ALU.subtract).then_inc(nm_done, 1)

            def add_rotated(m, b, l, q):
                need(dve, cos_done, m + 1)
                need(dve, sin_done, m + 1)
                nc.vector.tensor_tensor(t1[:, :], t1[:, :], t2[:, :], ALU.add).then_inc(rot_done, 1)

            def scale_norms(m, b, l, q):
                need(dve, rot_done, m + 1)
                need(dve, rn_done, m + 1)
                need(dve, qkt_mm, m)
                nc.vector.tensor_tensor(qk[:, :].rearrange("p (h d) -> p h d", d=DH),
                                        t1[:, :].rearrange("p (h d) -> p h d", d=DH),
                                        rn[:, b % 2, :].unsqueeze(2).broadcast_to([P, 2 * HEADS, DH]),
                                        ALU.mult).then_inc(qk_done, 1)

            def normalise_out(m, b, l, q):
                ps = p_qk[:, :].rearrange("p (a c) -> p a c", a=2)[:, :, 0:4 * VW].rearrange("p a (h d) -> p a h d", d=VW)
                need(dve, pv_mm, m + 1)
                need(dve, ot_mm, m - 1)
                need(dve, o_done, m)
                nc.vector.reciprocal(rden[:, :, :], ps[:, :, :, DH]).then_inc(rden_done, 1)
                need(dve, rden_done, m + 1)
                nc.vector.tensor_tensor(O[:, b % 2, :].rearrange("p (a h d) -> p a h d", a=2, h=4), ps[:, :, :, 0:DH],
                                        rden[:, :, :].unsqueeze(3).broadcast_to([P, 2, 4, DH]), ALU.mult).then_inc(o_done, 1)

            def add_attention(m, b, l, q):
                r = row_of(m, l)
                need(dve, wo_mm, m + 1)
                need(dve, ht_mm, capped(m + 2))
                nc.vector.tensor_tensor(x[:, r, :], x[:, r, :], p_small[:, 0:D], ALU.add).then_inc(wo_added, 1)

            def mlp_stats(s, l):
                need(dve, ms_in, 48 * (s + 1))
                for b in range(BLKS):
                    nc.vector.bn_stats(mst[:, b, :], ms[:, b, :]).then_inc(m_stats, 1)
                hold(dve, m_stats, s * 2 * BLKS + BLKS)
                for b in range(BLKS):
                    nc.vector.bn_aggr(mmv[:, b, :], mst[:, b, :]).then_inc(m_stats, 1)
                need(dve, m_stats, (s + 1) * 2 * BLKS)
                need(dve, m_norm, s)
                nc.vector.tensor_scalar(mrs[:, :], mmv[:, :, 1], EPS, None, ALU.add).then_inc(m_var, 1)

            def mlp_mean(s, l):
                need(dve, m_rstd, s + 1)
                nc.vector.scalar_tensor_tensor(mnm[:, :], mmv[:, :, 0], -1.0, mrs[:, :], ALU.mult, ALU.mult).then_inc(m_nmr, 1)

            def mlp_value(s, l, t):
                rows = min(P, HID - t * P)
                need(dve, up_mm, s * HT + t + 1)
                need(dve, down_mm, s)
                nc.vector.tensor_scalar(ha[0:rows, t, :], p_sim[0:rows, 0:512], b1[0:rows, l, 0, t:t + 1], None,
                                        ALU.add).then_inc(a_copied, 1)

            def mlp_hidden(s, l):
                need(dve, gelu_done, s + 1)
                need(dve, a_copied, (s + 1) * HT)
                nc.vector.tensor_tensor(ha[:, :, :], ha[:, :, :], hg[:, :, :], ALU.mult).then_inc(hid_done, 1)

            def mlp_add(s, l):
                q = s - l * SEQS
                need(dve, down_mm, s + 1)
                need(dve, b2_added, s + 1)
                xv = x[:, bass.ds(q * BLKS, BLKS), :]
                nc.vector.tensor_tensor(xv, xv, p_sim[:, 512:1024].rearrange("p (b d) -> p b d", b=BLKS),
                                        ALU.add).then_inc(mlp_added, 1)
                if l == LAYERS - 1:
                    need(dve, mlp_added, s + 1)
                    need(dve, x1_in, 16 * (q + 1))
                    nc.vector.tensor_tensor(xv, xv, x1[:, :, :], ALU.add).then_inc(fin_done, 1)

            def body(i, layer):
                up = seq_at(i, MLP_UP, layer)
                down = seq_at(i, MLP_DOWN, layer)
                for b in range(BLKS):
                    def do(step, lag):
                        at = block_at(i, b, lag, layer)
                        if at:
                            step(*at)

                    do(copy_maxima, LAG_SIM)
                    if b == 0 and up:
                        mlp_stats(*up)
                    do(cosine, LAG_PROJ)
                    do(maxima, LAG_MAX)
                    if b == 0 and up:
                        mlp_mean(*up)
                    do(sum_squares, LAG_PROJ)
                    do(normalise_out, LAG_PV)
                    do(add_rotated, LAG_PROJ)
                    do(scale_norms, LAG_PROJ)
                    do(add_attention, LAG_WO)
                    if b == 0 and down:
                        mlp_add(*down)
                    if b and up:
                        mlp_value(*up, b - 1)
                    if b == BLKS - 1 and up:
                        mlp_hidden(*up)

            iterate(dve, body)

        @block.gpsimd
        def _(pool):
            pool.memset(xs[0:1, 0, DH:D], 0.0).then_inc(init_done, 1)
            pool.memset(ms[0:1, 0, DH:D], 0.0).then_inc(init_done, 1)
            pool.memset(qz[:, :, :, :, :], 0.0).then_inc(init_done, 1)
            pool.memset(kT[:, :, 0:WINDOW], 0.0).then_inc(init_done, 1)
            pool.memset(kzb[:, :, :, :], 0.0).then_inc(init_done, 1)
            pool.memset(Vs[0:DH, 0, :, :], 0.0).then_inc(init_done, 1)
            pool.memset(V[:, :, :, DH:VW], 1.0).then_inc(init_done, 1)
            pool.memset(minus_half[:, :], -0.5).then_inc(init_done, 1)
            pool.memset(ha[:, HT - 1, :], 0.0).then_inc(init_done, 1)
            pool.memset(hg[:, HT - 1, :], 0.0).then_inc(init_done, 1)
            pool.wait_ge(w_in, 16 * N_WEIGHT_DMAS)
            pool.memset(R[:, :, :], 0.0).then_inc(init_done, 1)
            pool.wait_ge(init_done, N_INIT - 3)
            for v in range(2):
                nc.gpsimd.tensor_copy(R[0:WINDOW, :, v * WINDOW:(v + 1) * WINDOW],
                                      identb[0:WINDOW, 0:WINDOW].unsqueeze(1).broadcast_to([WINDOW, BLKS, WINDOW])).then_inc(init_done, 1)
            pool.memset(R[ROW_FIRST:ROW_FIRST + 1, 0, 0:WINDOW], 1.0).then_inc(init_done, 1)
            pool.wait_ge(tab_done, LAYERS)

            def sine(m, b, l, q):
                need(pool, u_copied, m + 1)
                need(pool, rot_done, m)
                half = DH // 2
                src = u[:, b % 2, :].rearrange("p (h a d) -> p h a d", a=2, d=half)
                dst = t2[:, :].rearrange("p (h a d) -> p h a d", a=2, d=half)
                for k in range(2):
                    t = tab[:, l, b, (2 + k) * DH:(3 + k) * DH].rearrange("p (a d) -> p a d", a=2)
                    heads = slice(k * HEADS, (k + 1) * HEADS)
                    for a in range(2):
                        last = nc.gpsimd.tensor_tensor(dst[:, heads, a, :], src[:, heads, 1 - a, :],
                                                       t[:, a, :].unsqueeze(1).broadcast_to([P, HEADS, half]), ALU.mult)
                last.then_inc(sin_done, 1)

            def to_bf16(m, b, l, q):
                need(pool, qkt_copied, m + 1)
                hold(pool, max_mm, m - 3)
                cols = slice(WINDOW + b * P, WINDOW + (b + 1) * P)
                nc.gpsimd.tensor_tensor(qb[:, b, :, :], qz[:, b, :, 0, :], qz[:, b, :, 1, :], ALU.add)
                for h in range(2):
                    last = nc.gpsimd.tensor_scalar(kzb[:, :, h, cols], kT[:, :, cols], halves[:, h:h + 1], 0.0, ALU.mult, ALU.add)
                last.then_inc(bf_done, 1)

            def norms(m, b, l, q):
                need(pool, clamped, m + 1)
                need(pool, qk_done, m - 1)
                nc.gpsimd.tensor_tensor(rn[:, b % 2, :], ss[:, b % 2, :], minus_half[:, :], ALU.pow).then_inc(rn_done, 1)

            def mlp_rstd(s, l):
                need(pool, m_var, s + 1)
                nc.gpsimd.tensor_tensor(mrs[:, :], mrs[:, :], minus_half[:, 0:BLKS], ALU.pow).then_inc(m_rstd, 1)

            def mlp_norm(s, l):
                need(pool, m_nmr, s + 1)
                hold(pool, m_tr, s)
                for b in range(BLKS):
                    last = nc.gpsimd.tensor_scalar(mln[:, b, :], ms[:, b, :], mrs[:, b:b + 1], mnm[:, b:b + 1], ALU.mult, ALU.add)
                last.then_inc(m_norm, 1)

            def add_b2(s, l):
                q = s - l * SEQS
                need(pool, ms_in, 48 * (s + 1))
                xv = x[:, bass.ds(q * BLKS, BLKS), :]
                nc.gpsimd.tensor_tensor(xv, xv, b2[:, l, :].unsqueeze(1).broadcast_to([P, BLKS, D]), ALU.add).then_inc(b2_added, 1)

            def body(i, layer):
                up = seq_at(i, MLP_UP, layer)
                for b in range(BLKS):
                    at = block_at(i, b, LAG_PROJ, layer)
                    if b == 0 and up:
                        mlp_rstd(*up)
                    if at:
                        sine(*at)
                        norms(*at)
                    if b == 0 and up:
                        mlp_norm(*up)
                        add_b2(*up)
                    at = block_at(i, b, LAG_QKT, layer)
                    if at:
                        to_bf16(*at)

            iterate(pool, body)


N_WEIGHT_DMAS = 13 + 6 + LAYERS * HT
N_INIT = 14


def ema_then_stack(nc, T):
    with ExitStack() as ctx:
        T["xcur"] = ctx.enter_context(nc.sbuf_tensor("xcur", [P, NBLK, D], F32))
        T["taps"] = nc.dram_tensor("taps_dram", [P, 2 * P], F32, kind="Internal").ap()
        T["x1"] = nc.dram_tensor("x1_dram", [SEQS, LEN, D], F32, kind="Internal").ap()
        ema_part(nc, T)
        stack_part(nc, T)


def shape_constants(np, bf16):
    f = np.float32
    half = np.arange(0, DH, 2, dtype=f)
    inv = (f(1.0) / f(10000.0) ** (half / f(DH))).astype(f)
    t = np.arange(LEN, dtype=f)
    fr = (t[:, None] * inv[None, :]).astype(f).astype(np.float64)
    fr = np.concatenate([fr, fr], 1)
    base = ((half + f(0.4 * DH)) / f(1.4 * DH)).astype(f)
    power = ((t - LEN // 2) / f(WINDOW // 2)).astype(f)
    sc = base.astype(np.float64)[None, :] ** power.astype(np.float64)[:, None]
    sc = np.concatenate([sc, sc], 1)
    sign = np.where(np.arange(DH) < DH // 2, -1.0, 1.0)
    rope = np.stack([QK_SCALE * np.cos(fr) * sc, np.cos(fr) / sc,
                     QK_SCALE * np.sin(fr) * sc * sign, np.sin(fr) / sc * sign], 1)
    rope = rope.reshape(BLKS, P, 4 * DH).transpose(1, 0, 2).astype(f)
    q = np.arange(P)[:, None] % WINDOW
    j = np.arange(P)[None, :]
    band = np.where((j < q) | (j > q + WINDOW), NEG, 0.0)
    first = np.where((np.arange(P)[:, None] < WINDOW) & (j < WINDOW), NEG, 0.0)
    mask_n = np.stack([band, band + first], 1).astype(bf16)
    mask_t = np.zeros((P, HEADS, P))
    mask_t[0:WINDOW] = band[0:WINDOW][:, None, :]
    for h in range(HEADS):
        mask_t[ROW_MAX + h, h] = 1.0
        mask_t[ROW_MAX + HEADS + h, h] = 1.0
    mask_t[ROW_FIRST, :, 0:WINDOW] = NEG
    ramp = np.concatenate([np.tile(np.arange(P), (P, 1)), np.tile(np.arange(1, P + 1), (P, 1)),
                           np.arange(P)[:, None]], 1).astype(f)
    return {"rope": np.ascontiguousarray(rope), "mask_n": mask_n, "mask_t": mask_t.astype(bf16),
            "ident": np.eye(P, dtype=f),
            "halves": np.repeat(np.eye(2, dtype=f), DH, 0), "identb": np.eye(P).astype(bf16), "ramp": ramp}


_ATTN = {"x": "x", "delta": "delta", "alpha": "alpha", "beta": "beta", "gamma": "gamma", "omega": "omega"}
_FFN = ["wqkv", "q_scale", "k_scale", "wo", "ln_g", "ln_b", "w1", "b1", "w2", "b2"]


def kernel(**inputs):
    import ml_dtypes
    import numpy as np
    import concourse.bacc as bacc
    from concourse.bass_utils import run_bass_kernel_spmd

    arrays = {name: np.ascontiguousarray(inputs[f"L0_attn_{name}"]) for name in _ATTN}
    for name in ("delta", "alpha", "beta"):
        arrays[name] = arrays[name].reshape(D, STATES)
    arrays["x_rev"] = np.ascontiguousarray(arrays["x"].reshape(SEQS, BLKS, P, D)[:, :, ::-1]).reshape(SEQS, LEN, D)
    arrays.update({name: np.ascontiguousarray(inputs[f"L0_ffn_{name}"]) for name in _FFN})
    for name in ("delta", "alpha", "beta", "gamma", "ln_g", "ln_b"):
        arrays[name + "_t"] = np.ascontiguousarray(arrays[name].T)
    b1 = np.zeros((LAYERS, 2, HT * P), arrays["b1"].dtype)
    b1[:, :, :HID] = arrays.pop("b1").reshape(LAYERS, 2, HID)
    arrays["b1_t"] = np.ascontiguousarray(b1.reshape(LAYERS, 2, HT, P).transpose(3, 0, 1, 2))
    arrays.update(shape_constants(np, ml_dtypes.bfloat16))
    nc = bacc.Bacc("TRN2", target_bir_lowering=False, num_devices=1)
    feed, T = {}, {}
    for name, a in arrays.items():
        feed[f"in_{name}_dram"] = a
        T[name] = nc.dram_tensor(f"in_{name}_dram", a.shape, mybir.dt.from_np(a.dtype), kind="ExternalInput").ap()
    T["out"] = nc.dram_tensor("out_dram", (SEQS, LEN, D), F32, kind="ExternalOutput").ap()
    ema_then_stack(nc, T)
    return run_bass_kernel_spmd(nc, [feed], core_ids=[0]).results[0]["out_dram"]
```

```python
from contextlib import ExitStack

import concourse.bass as bass
from concourse import mybir

F32 = mybir.dt.float32
F32R = mybir.dt.float32r
BF16 = mybir.dt.bfloat16
ALU = mybir.AluOpType
ACT = mybir.ActivationFunctionType
AX = mybir.AxisListType

P = 128
SEQS, LEN, D = 16, 512, 128
BLKS = LEN // P
NBLK = SEQS * BLKS
STATES = 16
LAYERS, HEADS, DH, WINDOW = 2, 8, 64, 64
PAIRS = HEADS // 2
INNER = HEADS * DH
HID = int(D * 4 * 2 / 3)
HT = -(-HID // P)
EPS = 1e-5
NORM_MIN = 1e-12
QK_SCALE = 8.0
NEG = -1e30
VW = DH + 1

CH = 8
GROUPS = D // CH

LAG_LOAD = 0
LAG_PROJ = 1
LAG_SCALE = 2
LAG_QKT = 2
LAG_MAX = 3
LAG_SIM = 4
LAG_PV = 5
LAG_OT = 6
LAG_WO = 7
MLP_IN = 2
MLP_UP = 3
MLP_DOWN = 4
X1_SEQS = (0, 1, 4, 8, SEQS)
X1_PIECES = len(X1_SEQS) - 1
HEAD_ITERS = 4
TOTAL = LAYERS * NBLK
ITERS = TOTAL // BLKS + HEAD_ITERS

ROW_MAX = 64
ROW_FIRST = 96


def ema_part(nc, T, W):
    ctx = ExitStack()
    with ctx:
        def sb(name, shape, dt=F32):
            return ctx.enter_context(nc.sbuf_tensor(name, shape, dt))

        def sem(name):
            return ctx.enter_context(nc.semaphore(name))

        X = W["x"]
        Xr = sb("Xr", [P, NBLK, D])
        Y = sb("Y", [P, D, NBLK])
        stats = sb("stats", [P, NBLK, 6])
        mv = sb("mv", [P, NBLK, 2])
        rstd = sb("rstd", [P, NBLK])
        nmr = sb("nmr", [P, NBLK])
        par_d = sb("par_d", [P, 4, STATES])
        om = sb("om", [P, 1])
        lnq_d = sb("lnq_d", [P, STATES])
        cf_d = sb("cf_d", [P, STATES])
        dec = sb("dec", [P, D * STATES])
        par_n = sb("par_n", [STATES, 4, D])
        lnq_n = sb("lnq_n", [STATES, D])
        cf_n = sb("cf_n", [STATES, D])
        q128 = sb("q128", [STATES, D])
        ramps = sb("ramps", [P, 2 * P + 1])
        ramp = ramps[:, 0:P]
        ramp1 = ramps[:, P:2 * P]
        age = ramps[:, 2 * P:2 * P + 1]
        kpad = sb("kpad", [P, 2 * P])
        ktmp = sb("ktmp", [P, 2, P])
        toep = sb("toep", [P, 2, CH, P])
        cexp = sb("cexp", [P, 2, CH, P])
        par_b = [t[:, :, :, :].rearrange("p a c t -> p (a c t)") for t in (toep, cexp)]
        S = sb("S", [STATES, 2, CH, NBLK])
        H = sb("H", [STATES, 2, CH, 3 * SEQS])
        stage = Xr[:, :, :].rearrange("p m d -> p (m d)")
        at = [0]

        def staged(*shape):
            n = 1
            for k in shape:
                n *= k
            at[0] += n
            return stage[:, at[0] - n:at[0]]

        wqkv_in = staged(LAYERS, 3 * INNER).rearrange("p (l n) -> p l n", l=LAYERS)
        w1_in = staged(LAYERS, 2, HID).rearrange("p (l g n) -> p l g n", l=LAYERS, g=2)
        rope = staged(BLKS, 4 * DH).rearrange("p (b n) -> p b n", b=BLKS)
        scl = staged(LAYERS, 4 * DH).rearrange("p (l n) -> p l n", l=LAYERS)
        pS = [ctx.enter_context(nc.psum_tensor(f"pS{i}", [P, 512], F32)) for i in range(2)]
        pO = [ctx.enter_context(nc.psum_tensor(f"pO{i}", [P, 512], F32)) for i in range(2)]

        xr_in = [sem(f"xr_in{i}") for i in range(4)]
        x_in = sem("x_in")
        da_in = sem("da_in")
        par_in = sem("par_in")
        stage_in = sem("stage_in")
        w_in = sem("w_in")
        stats_done = sem("stats_done")
        mv_done = sem("mv_done")
        var_done = sem("var_done")
        ln_done = sem("ln_done")
        rstd_done = sem("rstd_done")
        nmr_done = sem("nmr_done")
        y_done = sem("y_done")
        a_par = sem("a_par")
        prod_done = sem("prod_done")
        v_par = sem("v_par")
        coef_done = sem("coef_done")
        k_exp = sem("k_exp")
        k_acc = sem("k_acc")
        kpad_done = sem("kpad_done")
        k_zero = sem("k_zero")
        k_out = sem("k_out")
        toep_in = [sem(f"toep_in{i}") for i in range(2)]
        c_arg = sem("c_arg")
        c_done = sem("c_done")
        s_mm = sem("s_mm")
        h_step = sem("h_step")
        o_mm = sem("o_mm")
        x1_add = sem("x1_add")
        w_zero = sem("w_zero")
        w_hi = sem("w_hi")
        w_lo = sem("w_lo")
        tab_done = sem("tab_done")

        x_d = T["x"].rearrange("a (b p) d -> p (a b) d", p=P)
        xr_d = T["x_rev"].rearrange("a (b p) d -> p (a b) d", p=P)
        CHUNK = NBLK // 4
        Y_POOL, Y_DVE, Y_ACT = range(0, 31), range(31, 54), range(54, NBLK)

        def y_col(m):
            return (m % BLKS) * SEQS + m // BLKS

        block = ctx.enter_context(nc.Block())

        @block.sync
        def _(sp):
            for c in range(4):
                m = slice(c * CHUNK, (c + 1) * CHUNK)
                sp.dma_start(Xr[:, m, :], xr_d[:, m, :]).then_inc(xr_in[c], 16)
            half = DH // 2

            def load_weights():
                pieces = [(W["ident"][:, :], T["ident"]),
                          (W["identb"][:, :], T["identb"]),
                          (W["halves"][:, :], T["halves"]),
                          (W["mask_n"][:, :, :], T["mask_n"]),
                          (W["mask_t"][:, :, :], T["mask_t"]),
                          (W["wo"][:, :, :, :], T["wo"].rearrange("l (k p) n -> p l k n", p=P)),
                          (W["b1"][:, :, :, :], T["b1_t"]),
                          (W["lg"][:, :], T["ln_g_t"]),
                          (W["lb"][:, :], T["ln_b_t"]),
                          (W["b2"][:, :, :], bass.AP(tensor=T["b2"].tensor, offset=0, ap=[[0, P], [D, LAYERS], [1, D]]))]
                for l in range(LAYERS):
                    for t in range(HT):
                        rows = min(P, HID - t * P)
                        pieces.append((W["w2"][0:rows, l, t, :], T["w2"][l, t * P:t * P + rows, :]))
                for dst, src in pieces:
                    sp.dma_start(dst, src).then_inc(w_in, 16)
                return len(pieces)

            def load_staged():
                pieces = [(wqkv_in, T["wqkv"].rearrange("l p n -> p l n")),
                          (w1_in, T["w1"].rearrange("l p (g n) -> p l g n", g=2)),
                          (rope, T["rope"])]
                for k, name in enumerate(("q_scale", "k_scale")):
                    for to, frm, n in ((k * DH, 0, DH), ((2 + k) * DH, half, half), ((2 + k) * DH + half, 0, half)):
                        pieces.append((scl[:, :, to:to + n],
                                       bass.AP(tensor=T[name].tensor, offset=frm, ap=[[0, P], [DH, LAYERS], [1, n]])))
                assert len(pieces) == N_STAGED
                for dst, src in pieces:
                    sp.dma_start(dst, src).then_inc(stage_in, 16)

            sp.wait_ge(kpad_done, 1)
            sp.dma_start(T["taps"], kpad[:, :]).then_inc(k_out, 16)
            sp.wait_ge(k_out, 16)
            for g in range(GROUPS):
                if g >= 2:
                    sp.wait_ge(o_mm, g - 1)
                sp.dma_start(toep[:, g % 2], bass.AP(tensor=T["taps"].tensor, offset=g * CH * 2 * P + 1,
                                                     ap=[[1, P], [2 * P, CH], [1, P]])).then_inc(toep_in[g % 2], 16)
                if g == 1:
                    sp.dma_start(X[:, :, :], x_d).then_inc(x_in, 16)
                    sp.wait_ge(y_done, NBLK)
                    load_staged()
                if g == 2:
                    weights = load_weights()
            sp.wait_ge(w_in, 16 * weights)

        @block.scalar
        def _(act):
            for k, name in enumerate(("delta", "alpha", "beta", "gamma")):
                arrived = da_in if k < 2 else par_in
                flat = T[name].rearrange("d n -> (d n)")
                act.dma_start(par_d[:, k, :], T[name]).then_inc(arrived, 16)
                act.dma_start(par_n[:, k, :], T[name + "_t"]).then_inc(arrived, 16)
                if k < 2:
                    act.dma_start(par_b[k], bass.AP(tensor=flat.tensor, offset=0, ap=[[0, P], [1, D * STATES]])).then_inc(da_in, 16)
            act.dma_start(om[:, :], T["omega"].rearrange("(d a) -> d a", a=1)).then_inc(par_in, 16)
            act.dma_start(ramps[:, :], T["ramp"]).then_inc(par_in, 16)
            act.wait_ge(da_in, 16 * 6)
            nc.scalar.activation(par_d[:, 0:2, :], par_d[:, 0:2, :], ACT.Sigmoid).then_inc(a_par, 1)
            nc.scalar.activation(par_n[:, 0:2, :], par_n[:, 0:2, :], ACT.Sigmoid).then_inc(a_par, 1)
            nc.scalar.activation(par_b[0], par_b[0], ACT.Sigmoid).then_inc(a_par, 1)
            nc.scalar.activation(par_b[1], par_b[1], ACT.Sigmoid).then_inc(a_par, 1)
            act.wait_ge(v_par, 3)
            nc.scalar.activation(lnq_d[:, :], lnq_d[:, :], ACT.Ln).then_inc(a_par, 1)
            nc.scalar.activation(lnq_n[:, :], lnq_n[:, :], ACT.Ln).then_inc(a_par, 1)
            nc.scalar.activation(dec[:, :], dec[:, :], ACT.Ln).then_inc(a_par, 1)
            act.wait_ge(var_done, 1)
            nc.scalar.activation(rstd[:, :], rstd[:, :], ACT.Ln).then_inc(ln_done, 1)
            act.wait_ge(ln_done, 1)
            nc.scalar.activation(rstd[:, :], rstd[:, :], ACT.Exp, scale=-0.5).then_inc(rstd_done, 1)
            act.wait_ge(a_par, 7)
            act.wait_ge(par_in, 16 * 6)
            for n in range(STATES):
                if n >= 2:
                    act.wait_ge(k_acc, n - 1)
                nc.scalar.activation(ktmp[:, n % 2, :], ramp[:, :], ACT.Exp, scale=lnq_d[:, n:n + 1]).then_inc(k_exp, 1)
            nc.scalar.activation(q128[:, :], lnq_n[:, :], ACT.Exp, scale=float(P)).then_inc(a_par, 1)
            nc.scalar.activation(dec[:, :], dec[:, :], ACT.Exp, scale=age[:, 0:1]).then_inc(a_par, 1)
            act.wait_ge(nmr_done, 1)
            for m in Y_ACT:
                nc.scalar.activation(Y[:, :, y_col(m)], Xr[:, m, :], ACT.Identity, bias=nmr[:, m:m + 1],
                                     scale=rstd[:, m:m + 1]).then_inc(y_done, 1)
            for g in range(GROUPS):
                act.wait_ge(c_arg, g + 1)
                nc.scalar.activation(cexp[0:STATES, g % 2], cexp[0:STATES, g % 2], ACT.Exp).then_inc(c_done, 1)
                if g == 2:
                    act.wait_ge(stage_in, 16 * N_STAGED)
                    act.wait_ge(w_zero, 2)
                    nc.scalar.activation(W["wqkv"][:, 0], wqkv_in, ACT.Copy).then_inc(w_hi, 1)
                    nc.scalar.activation(W["w1"][:, 0, :, :, 0:HID], w1_in, ACT.Copy).then_inc(w_hi, 1)

        @block.gpsimd
        def _(pool):
            for part in range(2):
                pool.memset(W["w1"][:, part].bitcast(F32), 0.0).then_inc(w_zero, 1)
            pool.wait_ge(nmr_done, 1)
            for m in Y_POOL:
                nc.gpsimd.tensor_scalar(Y[:, :, y_col(m)], Xr[:, m, :], rstd[:, m:m + 1], nmr[:, m:m + 1],
                                        ALU.mult, ALU.add).then_inc(y_done, 1)

        @block.vector
        def _(dve):
            nc.vector.memset(kpad[:, :], 0.0).then_inc(k_zero, 1)

            def chunk_stats(c):
                dve.wait_ge(xr_in[c], 16)
                for m in range(c * CHUNK, (c + 1) * CHUNK):
                    nc.vector.bn_stats(stats[:, m, :], Xr[:, m, :]).then_inc(stats_done, 1)
                dve.wait_ge(stats_done, (c + 1) * CHUNK)
                for m in range(c * CHUNK, (c + 1) * CHUNK):
                    nc.vector.bn_aggr(mv[:, m, :], stats[:, m, :]).then_inc(mv_done, 1)

            chunk_stats(0)
            chunk_stats(1)
            chunk_stats(2)
            dve.wait_ge(a_par, 4)
            for k, (q, a, b) in enumerate(((lnq_d[:, :], par_d[:, 0, :], par_d[:, 1, :]),
                                           (lnq_n[:, :], par_n[:, 0, :], par_n[:, 1, :]),
                                           (dec[:, :], par_b[0], par_b[1]))):
                nc.vector.tensor_tensor(q, a, b, ALU.mult).then_inc(prod_done, 1)
                dve.wait_ge(prod_done, k + 1)
                nc.vector.tensor_scalar(q, q, -1.0, 1.0, ALU.mult, ALU.add).then_inc(v_par, 1)
            chunk_stats(3)
            dve.wait_ge(mv_done, NBLK)
            nc.vector.tensor_scalar(rstd[:, :], mv[:, :, 1], EPS, None, ALU.add).then_inc(var_done, 1)
            dve.wait_ge(par_in, 16 * 6)
            for k, (c, par) in enumerate(((cf_d[:, :], par_d), (cf_n[:, :], par_n))):
                nc.vector.tensor_tensor(c, par[:, 0, :], par[:, 2, :], ALU.mult).then_inc(coef_done, 1)
                dve.wait_ge(coef_done, 2 * k + 1)
                nc.vector.scalar_tensor_tensor(c, c, float(STATES) ** -0.5, par[:, 3, :],
                                               ALU.mult, ALU.mult).then_inc(coef_done, 1)
            dve.wait_ge(coef_done, 4)
            dve.wait_ge(rstd_done, 1)
            nc.vector.scalar_tensor_tensor(nmr[:, :], mv[:, :, 0], -1.0, rstd[:, :],
                                           ALU.mult, ALU.mult).then_inc(nmr_done, 1)
            dve.wait_ge(k_zero, 1)
            for n in range(STATES):
                dve.wait_ge(k_exp, n + 1)
                if n:
                    dve.wait_ge(k_acc, n)
                nc.vector.scalar_tensor_tensor(kpad[:, P:2 * P], ktmp[:, n % 2, :], cf_d[:, n:n + 1],
                                               kpad[:, P:2 * P], ALU.mult, ALU.add).then_inc(k_acc, 1)
            dve.wait_ge(k_acc, STATES)
            nc.vector.tensor_tensor(kpad[:, P:P + 1], kpad[:, P:P + 1], om[:, :], ALU.add).then_inc(kpad_done, 1)
            dve.wait_ge(nmr_done, 1)
            for m in Y_DVE:
                nc.vector.tensor_scalar(Y[:, :, y_col(m)], Xr[:, m, :], rstd[:, m:m + 1], nmr[:, m:m + 1],
                                        ALU.mult, ALU.add).then_inc(y_done, 1)

            def state_arguments(g):
                if g >= 2:
                    dve.wait_ge(o_mm, g - 1)
                nc.vector.tensor_tensor(
                    cexp[0:STATES, g % 2], lnq_n[:, g * CH:g * CH + CH].unsqueeze(2).broadcast_to([STATES, CH, P]),
                    ramp1[0:STATES, :].unsqueeze(1).broadcast_to([STATES, CH, P]), ALU.mult).then_inc(c_arg, 1)

            def carry_states(g):
                if g >= 2:
                    dve.wait_ge(o_mm, g - 1)
                dve.wait_ge(s_mm, g + 1)
                s = S[:, g % 2]
                h = H[:, g % 2]
                cf = cf_n[:, g * CH:g * CH + CH].unsqueeze(2).broadcast_to([STATES, CH, NBLK])
                qq = q128[:, g * CH:g * CH + CH].unsqueeze(2).broadcast_to([STATES, CH, SEQS])
                nc.vector.tensor_tensor(s, pS[g % 2][0:STATES, :].rearrange("p (c m) -> p c m", c=CH), cf,
                                        ALU.mult).then_inc(h_step, 1)
                dve.wait_ge(h_step, 6 * g + 1)
                nc.vector.tensor_copy(h[:, :, 0:SEQS], s[:, :, 0:SEQS]).then_inc(h_step, 1)
                for j in (1, 2):
                    dve.wait_ge(h_step, 6 * g + 2 * j)
                    nc.vector.tensor_tensor(h[:, :, j * SEQS:(j + 1) * SEQS], h[:, :, (j - 1) * SEQS:j * SEQS], qq,
                                            ALU.mult).then_inc(h_step, 1)
                    dve.wait_ge(h_step, 6 * g + 2 * j + 1)
                    nc.vector.tensor_tensor(h[:, :, j * SEQS:(j + 1) * SEQS], h[:, :, j * SEQS:(j + 1) * SEQS],
                                            s[:, :, j * SEQS:(j + 1) * SEQS], ALU.add).then_inc(h_step, 1)

            def add_out(g):
                dve.wait_ge(o_mm, g + 1)
                xv = X[:, :, g * CH:(g + 1) * CH].rearrange("p (s b) d -> p d b s", b=BLKS)
                ov = pO[g % 2][:, :].rearrange("p (d b s) -> p d b s", d=CH, b=BLKS)
                for b in range(BLKS):
                    last = nc.vector.tensor_tensor(xv[:, :, b], xv[:, :, b], ov[:, :, b], ALU.add)
                last.then_inc(x1_add, 1)

            dve.wait_ge(a_par, 9)
            for g in range(GROUPS + 2):
                if g < GROUPS:
                    state_arguments(g)
                if 1 <= g <= GROUPS:
                    carry_states(g - 1)
                if g >= 2:
                    if g == 2:
                        dve.wait_ge(x_in, 16)
                    add_out(g - 2)
                if g == 4:
                    dve.wait_ge(w_hi, 1)
                    nc.vector.tensor_tensor(W["wqkv"][:, 1], wqkv_in, W["wqkv"][:, 0].bitcast(F32), ALU.subtract).then_inc(w_lo, 1)
                if g == 5:
                    dve.wait_ge(w_hi, 2)
                    for l in range(LAYERS):
                        nc.vector.tensor_tensor(W["w1"][:, 1, l, :, 0:HID], w1_in[:, l], W["w1"][:, 0, l, :, 0:HID].bitcast(F32),
                                                ALU.subtract).then_inc(w_lo, 1)
                if g == 6:
                    dve.wait_ge(stage_in, 16 * N_STAGED)
                    for l in range(LAYERS):
                        nc.vector.tensor_tensor(W["tab"][:, l], rope, scl[:, l, :].unsqueeze(1).broadcast_to([P, BLKS, 4 * DH]),
                                                ALU.mult).then_inc(tab_done, 1)
            dve.wait_ge(x1_add, GROUPS)
            dve.wait_ge(w_lo, 3)
            dve.wait_ge(tab_done, LAYERS)

        @block.tensor
        def _(pe):
            decays = dec[:, :].rearrange("p (d n) -> p d n", d=D)
            pe.wait_ge(a_par, 9)
            pe.wait_ge(y_done, NBLK)

            def states(g):
                if g >= 2:
                    pe.wait_ge(h_step, 6 * (g - 2) + 1)
                for c in range(CH):
                    last = nc.tensor.matmul(pS[g % 2][0:STATES, c * NBLK:(c + 1) * NBLK], decays[:, g * CH + c, :],
                                            Y[:, g * CH + c, :], start=True, stop=True)
                last.then_inc(s_mm, 1)

            def outputs(g):
                pe.wait_ge(toep_in[g % 2], 16 * (g // 2 + 1))
                if g >= 2:
                    pe.wait_ge(x1_add, g - 1)
                for c in range(CH):
                    last = nc.tensor.matmul(pO[g % 2][:, c * NBLK:(c + 1) * NBLK], toep[:, g % 2, c, :],
                                            Y[:, g * CH + c, :], start=(c == 0), stop=False, skip_group_check=True)
                pe.wait_ge(c_done, g + 1)
                pe.wait_ge(h_step, 6 * g + 6)
                for c in range(CH):
                    last = nc.tensor.matmul(pO[g % 2][:, c * NBLK + SEQS:(c + 1) * NBLK], cexp[0:STATES, g % 2, c, :],
                                            H[:, g % 2, c, :], start=False, stop=(c == CH - 1), skip_group_check=True)
                last.then_inc(o_mm, 1)

            states(0)
            for g in range(GROUPS):
                if g + 1 < GROUPS:
                    states(g + 1)
                outputs(g)


def stack_weights(nc, ctx):
    shapes = {"x": ([P, NBLK, D], F32),
              "wqkv": ([P, 2, LAYERS, 3 * INNER], F32R),
              "w1": ([P, 2, LAYERS, 2, HT * P], F32R),
              "wo": ([P, LAYERS, PAIRS, D], F32),
              "w2": ([P, LAYERS, HT, D], F32),
              "b1": ([P, LAYERS, 2, HT], F32),
              "b2": ([P, LAYERS, D], F32),
              "lg": ([P, LAYERS], F32),
              "lb": ([P, LAYERS], F32),
              "tab": ([P, LAYERS, BLKS, 4 * DH], F32),
              "ident": ([P, P], F32),
              "halves": ([P, 2], F32),
              "identb": ([P, P], BF16),
              "mask_n": ([P, 2, P], BF16),
              "mask_t": ([P, HEADS, P], BF16)}
    return {name: ctx.enter_context(nc.sbuf_tensor(name, shape, dt)) for name, (shape, dt) in shapes.items()}


def stack_part(nc, T, W):
    ctx = ExitStack()
    with ctx:
        def sb(name, shape, dt=F32):
            return ctx.enter_context(nc.sbuf_tensor(name, shape, dt))

        def sem(name):
            return ctx.enter_context(nc.semaphore(name))

        x, wqkv, w1, wo, w2, b1, b2 = (W[k] for k in ("x", "wqkv", "w1", "wo", "w2", "b1", "b2"))
        lg, lb, tab, ident, halves, identb = (W[k] for k in ("lg", "lb", "tab", "ident", "halves", "identb"))
        mask_n, mask_t = W["mask_n"], W["mask_t"]

        xs = sb("xs", [P, BLKS, D])
        hT = sb("hT", [P, 2, 2, P], F32R)
        u = sb("u", [P, 2 * INNER])
        sq = sb("sq", [P, 2 * INNER])
        ss = sb("ss", [P, 2, 2 * HEADS])
        rn = sb("rn", [P, 2, 2 * HEADS])
        minus_half = sb("minus_half", [P, 2 * HEADS])
        t1 = sb("t1", [P, 2 * INNER])
        t2 = sb("t2", [P, 2 * INNER])
        qk = sb("qk", [P, 2 * INNER])
        qz = sb("qz", [P, BLKS, PAIRS, 2, P])
        kT = sb("kT", [P, PAIRS, WINDOW + LEN])
        qb = sb("qb", [P, BLKS, PAIRS, P], BF16)
        kzb = sb("kzb", [P, PAIRS, 2, WINDOW + LEN], BF16)
        nmax = sb("nmax", [P, HEADS])
        nm2 = sb("nm2", [P, 2, 2 * HEADS], BF16)
        R = sb("R", [P, BLKS, P], BF16)
        pT = sb("pT", [P, 2, HEADS, P])
        V = sb("V", [P, BLKS, HEADS, VW])
        Vs = sb("Vs", [P, BLKS, HEADS, VW])
        rden = sb("rden", [P, 2, PAIRS])
        O = sb("O", [P, 2, INNER])
        OT = sb("OT", [P, 2, PAIRS, P])
        ms = sb("ms", [P, BLKS, D])
        zst = sb("zst", [P, BLKS, 6])
        zmv = sb("zmv", [P, BLKS, 2])
        zrs = sb("zrs", [P, BLKS])
        znm = sb("znm", [P, BLKS])
        mst = sb("mst", [P, BLKS, 6])
        mmv = sb("mmv", [P, BLKS, 2])
        mrs = sb("mrs", [P, BLKS])
        mnm = sb("mnm", [P, BLKS])
        mln = sb("mln", [P, BLKS, D])
        h2 = sb("h2", [P, LEN])
        h2T = sb("h2T", [P, 2, LEN], F32R)
        ha = sb("ha", [P, HT, LEN])
        hg = sb("hg", [P, HT, LEN])
        x1 = sb("x1", [P, BLKS, D])

        def bank(name, n=1):
            return ctx.enter_context(nc.psum_tensor(name, [P, 512 * n], F32))

        p_qk = bank("p_qk", 2)
        p_v = bank("p_v")
        p_small = bank("p_small")
        p_max = bank("p_max", 2)
        p_sim = bank("p_sim", 2)

        init_done = sem("init_done")
        x1_out = [sem(f"x1_out{c}") for c in range(X1_PIECES)]
        z_stats = sem("z_stats")
        z_var = sem("z_var")
        z_rstd = sem("z_rstd")
        z_nmr = sem("z_nmr")
        z_done = sem("z_done")
        xs_in = [sem(f"xs_in{b}") for b in range(BLKS)]
        vs_in = [sem(f"vs_in{b}") for b in range(BLKS)]
        ms_in = sem("ms_in")
        x1_in = sem("x1_in")
        out_done = sem("out_done")
        mt_mm = sem("mt_mm")
        mt_copied = sem("mt_copied")
        qk_mm = sem("qk_mm")
        u_copied = sem("u_copied")
        squared = sem("squared")
        ss_done = sem("ss_done")
        clamped = sem("clamped")
        rn_done = sem("rn_done")
        cos_done = sem("cos_done")
        sin_done = sem("sin_done")
        rot_done = sem("rot_done")
        qk_done = sem("qk_done")
        qkt_mm = sem("qkt_mm")
        kt_copied = sem("kt_copied")
        qkt_copied = sem("qkt_copied")
        bf_done = sem("bf_done")
        max_mm = sem("max_mm")
        max_done = sem("max_done")
        nm_hi = sem("nm_hi")
        nm_done = sem("nm_done")
        sim_mm = sem("sim_mm")
        exp_done = sem("exp_done")
        ht_mm = sem("ht_mm")
        ht_hi = sem("ht_hi")
        ht_copied = sem("ht_copied")
        pv_mm = sem("pv_mm")
        rden_done = sem("rden_done")
        o_done = sem("o_done")
        v_mm = sem("v_mm")
        v_copied = sem("v_copied")
        ot_mm = sem("ot_mm")
        ot_copied = sem("ot_copied")
        wo_mm = sem("wo_mm")
        wo_added = sem("wo_added")
        m_stats = sem("m_stats")
        m_var = sem("m_var")
        m_rstd = sem("m_rstd")
        m_nmr = sem("m_nmr")
        m_norm = sem("m_norm")
        b2_added = sem("b2_added")
        m_tr = sem("m_tr")
        m_trc = sem("m_trc")
        h2_hi = sem("h2_hi")
        h2_done = sem("h2_done")
        up_mm = sem("up_mm")
        g_copied = sem("g_copied")
        a_copied = sem("a_copied")
        gelu_done = sem("gelu_done")
        hid_done = sem("hid_done")
        down_mm = sem("down_mm")
        mlp_added = sem("mlp_added")
        fin_done = sem("fin_done")
        held = sem("held")

        def iterate(eng, body):
            per_layer = SEQS
            for i in range(HEAD_ITERS):
                body(i, None)
            with eng.Fori(HEAD_ITERS, per_layer - 1) as i:
                body(i, 0)
            for i in range(per_layer - 1, per_layer + HEAD_ITERS):
                body(i, None)
            with eng.Fori(per_layer + HEAD_ITERS, 2 * per_layer) as i:
                body(i, 1)
            for i in range(2 * per_layer, ITERS):
                body(i, None)

        def block_at(i, b, lag, layer):
            m = i * BLKS + (b - lag)
            q = i + (b - lag) // BLKS
            if layer is None:
                return (m, m % BLKS, m // NBLK, q) if 0 <= m < TOTAL else None
            return m, (b - lag) % BLKS, layer, q

        def seq_at(i, lag, layer):
            s = i - lag
            if layer is None:
                return (s, s // SEQS) if 0 <= s < TOTAL // BLKS else None
            return s, layer

        def norm_at(i, layer):
            if layer is None:
                return i + 1 if i + 1 < SEQS else None
            return None if layer else i + 1

        def need(eng, semaphore, count):
            if not isinstance(count, int) or count > 0:
                eng.wait_ge(semaphore, count)

        def hold(eng, semaphore, count):
            need(eng, semaphore, count)
            if not isinstance(count, int):
                eng.sem_inc(held, 1)

        def capped(count):
            return min(count, TOTAL) if isinstance(count, int) else count

        def row_of(m, layer):
            return m - layer * NBLK

        x1_d = T["x1"].rearrange("a (b p) d -> p (a b) d", p=P)
        out_d = T["out"].rearrange("a (b p) d -> p (a b) d", p=P)
        block = ctx.enter_context(nc.Block())

        @block.sync
        def _(sp):
            def x1_to_dram(c):
                m = slice(X1_SEQS[c] * BLKS, X1_SEQS[c + 1] * BLKS)
                sp.dma_start(x1_d[:, m, :], x[:, m, :]).then_inc(x1_out[c], 16)

            x1_to_dram(0)
            sp.wait_ge(init_done, N_INIT_DMA)

            def shift_in(m, b, l, q):
                hold(sp, ht_mm, m - 3)
                if l:
                    hold(sp, mlp_added, q - SEQS + 1)
                else:
                    hold(sp, z_done, q + 1)
                r = row_of(m, l)
                sp.dma_start(xs[:, b, 0:DH], x[:, r, 0:DH]).then_inc(xs_in[b], 16)
                sp.dma_start(xs[1:P, b, DH:D], x[0:P - 1, r, DH:D]).then_inc(xs_in[b], 16)
                if b:
                    sp.dma_start(xs[0:1, b, DH:D], x[P - 1:P, r - 1, DH:D]).then_inc(xs_in[b], 16)

            def shift_v(m, b, l, q):
                hold(sp, v_copied, m + 1)
                hold(sp, pv_mm, m - 3)
                sp.dma_start(Vs[DH:P, b, :, :], V[0:DH, b, :, :]).then_inc(vs_in[b], 16)
                if b:
                    sp.dma_start(Vs[0:DH, b, :, :], V[DH:P, b - 1, :, :]).then_inc(vs_in[b], 16)

            def mlp_in(s, l):
                hold(sp, wo_added, (s + 1) * BLKS)
                hold(sp, m_norm, s)
                r = (s - l * SEQS) * BLKS
                sp.dma_start(ms[:, :, 0:DH], x[:, bass.ds(r, BLKS), 0:DH]).then_inc(ms_in, 16)
                sp.dma_start(ms[1:P, :, DH:D], x[0:P - 1, bass.ds(r, BLKS), DH:D]).then_inc(ms_in, 16)
                sp.dma_start(ms[0:1, 1:BLKS, DH:D], x[P - 1:P, bass.ds(r, BLKS - 1), DH:D]).then_inc(ms_in, 16)

            def final(s, l):
                q = s - l * SEQS
                hold(sp, fin_done, q + 1)
                sp.dma_start(out_d[:, bass.ds(q * BLKS, BLKS), :], x[:, bass.ds(q * BLKS, BLKS), :]).then_inc(out_done, 16)

            def load_x1(s, l):
                q = s - l * SEQS
                hold(sp, fin_done, q)
                sp.dma_start(x1[:, :, :], x1_d[:, bass.ds(q * BLKS, BLKS), :]).then_inc(x1_in, 16)

            def body(i, layer):
                for b in range(BLKS):
                    at = block_at(i, b, LAG_LOAD, layer)
                    if at:
                        shift_in(*at)
                    if b == BLKS - 1:
                        at = seq_at(i, MLP_IN, layer)
                        if at:
                            mlp_in(*at)
                    at = block_at(i, b, LAG_PROJ + 1, layer)
                    if at:
                        shift_v(*at)
                    if b == 0 and isinstance(i, int) and i + 1 < X1_PIECES:
                        x1_to_dram(i + 1)
                    if b == 1:
                        at = seq_at(i, MLP_DOWN, layer)
                        if at and at[1] == LAYERS - 1:
                            final(*at)
                        at = seq_at(i, MLP_UP, layer)
                        if at and at[1] == LAYERS - 1:
                            load_x1(*at)

            iterate(sp, body)
            for c in range(X1_PIECES):
                sp.wait_ge(x1_out[c], 16)
            sp.wait_ge(out_done, 16 * SEQS)

        @block.tensor
        def _(pe):
            def split_product(out, weights, moving):
                for k, (a, b) in enumerate(((0, 0), (0, 1), (1, 0))):
                    last = nc.tensor.matmul(out, weights(a), moving(b), start=(k == 0), stop=(k == 2))
                return last

            def transpose_maxima(m, b, l, q):
                need(pe, nm_done, m + 1)
                need(pe, wo_added, m - (LAG_WO - LAG_MAX) + 1)
                need(pe, ht_copied, capped(m + (LAG_MAX - LAG_LOAD) + 1))
                nc.tensor.transpose(p_small[0:2 * HEADS, 0:DH].bitcast(BF16), nm2[:, b % 2], identb[:, :]).then_inc(mt_mm, 1)

            def project_qk(m, b, l, q):
                need(pe, ht_copied, m + 1)
                need(pe, o_done, m - (LAG_PV - LAG_PROJ))
                need(pe, u_copied, m)
                for j in range(2):
                    last = split_product(p_qk[:, j * 512:(j + 1) * 512], lambda part: hT[:, b % 2, part, :],
                                         lambda part: wqkv[:, part, l, j * INNER:(j + 1) * INNER])
                last.then_inc(qk_mm, 1)

            def score_maxima(m, b, l, q):
                if isinstance(m, int) and m == 0:
                    pe.wait_ge(init_done, N_INIT)
                need(pe, qkt_copied, m + 1)
                need(pe, bf_done, m + 1)
                need(pe, qkt_copied, capped(m + (LAG_MAX - LAG_QKT)))
                need(pe, max_done, m)
                for j in range(2):
                    nc.tensor.matmul(p_max[:, j * 512:(j + 1) * 512], identb[:, :],
                                     mask_n[:, 1 if b == 0 else 0, :].unsqueeze(1).broadcast_to([P, 4, P]),
                                     start=True, stop=False, skip_group_check=True)
                for v in range(2):
                    for p in range(PAIRS):
                        key = (2 * b + v) * WINDOW
                        last = nc.tensor.matmul(p_max[v * 64:v * 64 + 64, p * 256:(p + 1) * 256],
                                                qb[:, b, p, v * WINDOW:(v + 1) * WINDOW],
                                                kzb[:, p, :, key:key + 2 * WINDOW],
                                                start=False, stop=True, skip_group_check=True)
                last.then_inc(max_mm, 1)

            def score(m, b, l, q):
                if isinstance(m, int) and m == 0:
                    pe.wait_ge(init_done, N_INIT)
                need(pe, mt_copied, m + 1)
                need(pe, exp_done, m)
                for h in range(HEADS):
                    nc.tensor.matmul(p_sim[:, h * P:(h + 1) * P], mask_t[:, h, :], R[:, b, :],
                                     start=(h % 4 == 0), stop=False, skip_group_check=True)
                heads = p_sim[:, :].rearrange("p (h q) -> p h q", h=HEADS)
                for p in range(PAIRS):
                    for v in range(2):
                        key = (2 * b + v) * WINDOW
                        cols = slice(v * WINDOW, (v + 1) * WINDOW)
                        last = nc.tensor.matmul(heads[:, 2 * p:2 * p + 2, cols], kT[:, p, key:key + 2 * WINDOW],
                                                qz[:, b, p, :, cols], start=False, stop=True, skip_group_check=True)
                last.then_inc(sim_mm, 1)

            def transpose_input(m, b, l, q):
                need(pe, xs_in[b], 16 * (3 if b else 2) * (q + 1))
                need(pe, mt_copied, m - (LAG_MAX - LAG_LOAD))
                need(pe, ht_copied, m)
                nc.tensor.transpose(p_small[:, 0:P], xs[:, b, :], ident[:, :]).then_inc(ht_mm, 1)

            def values(m, b, l, q):
                need(pe, u_copied, capped(m + (LAG_PV - LAG_PROJ) + 1))
                need(pe, o_done, m)
                need(pe, exp_done, m + 1)
                need(pe, vs_in[b], 16 * (2 if b else 1) * (q + 1))
                for v, vals in ((0, Vs), (1, V)):
                    for h in range(HEADS):
                        at = (h // 4) * 512 + (h % 4) * VW
                        last = nc.tensor.matmul(p_qk[v * 64:v * 64 + 64, at:at + VW],
                                                pT[:, b % 2, h, v * WINDOW:(v + 1) * WINDOW],
                                                vals[:, b, h, :], start=True, stop=True)
                last.then_inc(pv_mm, 1)

            def project_v(m, b, l, q):
                need(pe, ot_copied, m - (LAG_OT - LAG_PROJ))
                need(pe, v_copied, m)
                last = split_product(p_v[:, :], lambda part: hT[:, b % 2, part, :],
                                     lambda part: wqkv[:, part, l, 2 * INNER:3 * INNER])
                last.then_inc(v_mm, 1)

            def transpose_qk(m, b, l, q):
                need(pe, qk_done, m + 1)
                need(pe, max_done, m - (LAG_MAX - LAG_QKT) + 1)
                need(pe, qkt_copied, m)
                for t in range(2 * PAIRS):
                    last = nc.tensor.transpose(p_max[:, t * P:(t + 1) * P], qk[:, t * P:(t + 1) * P], ident[:, :])
                last.then_inc(qkt_mm, 1)

            def project_out(m, b, l, q):
                need(pe, ot_copied, m + 1)
                need(pe, mt_copied, capped(m + (LAG_WO - LAG_MAX)))
                need(pe, ht_copied, capped(m + (LAG_WO - LAG_LOAD) + 1))
                need(pe, wo_added, m)
                for p in range(PAIRS):
                    last = nc.tensor.matmul(p_small[:, 0:D], OT[:, b % 2, p, :], wo[:, l, p, :],
                                            start=(p == 0), stop=(p == PAIRS - 1))
                last.then_inc(wo_mm, 1)

            def transpose_out(m, b, l, q):
                need(pe, o_done, m + 1)
                need(pe, v_copied, capped(m + (LAG_OT - LAG_PROJ) + 1))
                need(pe, ot_copied, m)
                for p in range(PAIRS):
                    last = nc.tensor.transpose(p_v[:, p * P:(p + 1) * P], O[:, b % 2, p * P:(p + 1) * P], ident[:, :])
                last.then_inc(ot_mm, 1)

            def mlp_down(s, l):
                need(pe, hid_done, 2 * (s + 1))
                for b in range(BLKS):
                    for t in range(HT):
                        rows = min(P, HID - t * P)
                        last = nc.tensor.matmul(p_sim[:, 512 + b * D:512 + (b + 1) * D],
                                                ha[0:rows, t, b * P:(b + 1) * P], w2[0:rows, l, t, :],
                                                start=(t == 0), stop=(t == HT - 1))
                last.then_inc(down_mm, 1)

            def mlp_transpose(s, l):
                need(pe, m_norm, s + 1)
                for b in range(BLKS):
                    last = nc.tensor.transpose(p_sim[:, b * P:(b + 1) * P], mln[:, b, :], ident[:, :])
                last.then_inc(m_tr, 1)

            def mlp_up(s, l, t):
                need(pe, h2_done, s + 1)
                for g in range(2):
                    last = split_product(p_sim[:, g * 512:(g + 1) * 512],
                                         lambda part: w1[:, part, l, g, t * P:(t + 1) * P], lambda part: h2T[:, part, :])
                last.then_inc(up_mm, 1)

            def mlp_has_left(i, b, layer):
                if b == 0:
                    i, b = i - 1, BLKS
                up = seq_at(i, MLP_UP, layer)
                down = seq_at(i, MLP_DOWN, layer)
                if b == 1:
                    if down:
                        need(pe, mlp_added, down[0] + 1)
                    if up:
                        need(pe, m_trc, up[0] + 1)
                elif up:
                    need(pe, g_copied, up[0] * HT + b - 1)
                    need(pe, a_copied, up[0] * HT + b - 1)

            def body(i, layer):
                up = seq_at(i, MLP_UP, layer)
                down = seq_at(i, MLP_DOWN, layer)
                for b in range(BLKS):
                    def do(step, lag):
                        at = block_at(i, b, lag, layer)
                        if at:
                            step(*at)
                        return at

                    do(project_qk, LAG_PROJ)
                    do(transpose_input, LAG_LOAD)
                    mlp_has_left(i, b, layer)
                    sim = do(score, LAG_SIM)
                    do(score_maxima, LAG_MAX)
                    do(values, LAG_PV)
                    do(project_v, LAG_PROJ)
                    do(project_out, LAG_WO)
                    if sim and (up or down):
                        need(pe, exp_done, sim[0] + 1)
                    if b == 0:
                        if down:
                            mlp_down(*down)
                        if up:
                            mlp_transpose(*up)
                    elif up:
                        mlp_up(*up, b - 1)
                    do(transpose_qk, LAG_QKT)
                    do(transpose_maxima, LAG_MAX)
                    do(transpose_out, LAG_OT)

            iterate(pe, body)

        @block.scalar
        def _(act):
            def copy_input(m, b, l, q):
                need(act, ht_mm, m + 1)
                need(act, v_mm, m - 1)
                nc.scalar.activation(hT[:, b % 2, 0, :], p_small[:, 0:P], ACT.Copy).then_inc(ht_hi, 1)

            def copy_qk(m, b, l, q):
                need(act, qk_mm, m + 1)
                need(act, cos_done, m)
                need(act, sin_done, m)
                need(act, squared, m)
                nc.scalar.activation(u[:, :], p_qk[:, :], ACT.Copy).then_inc(u_copied, 1)

            def square(m, b, l, q):
                need(act, u_copied, m + 1)
                need(act, ss_done, m)
                nc.scalar.activation(sq[:, :], u[:, :], ACT.Square).then_inc(squared, 1)

            def softmax_exp(m, b, l, q):
                need(act, sim_mm, m + 1)
                need(act, pv_mm, m - 1)
                nc.scalar.activation(pT[:, b % 2], p_sim[:, :].rearrange("p (h q) -> p h q", h=HEADS), ACT.Exp).then_inc(exp_done, 1)

            def copy_v(m, b, l, q):
                need(act, v_mm, m + 1)
                need(act, pv_mm, m - 3)
                need(act, vs_in[(b - 3) % BLKS], 16 * (2 if (b - 3) % BLKS else 1) * (q + (b - 3) // BLKS + 1))
                nc.scalar.activation(V[:, b, :, 0:DH], p_v[:, :].rearrange("p (h d) -> p h d", h=HEADS), ACT.Copy).then_inc(v_copied, 1)

            def copy_qkt(m, b, l, q):
                if isinstance(m, int) and m == 0:
                    act.wait_ge(init_done, N_INIT)
                need(act, qkt_mm, m + 1)
                need(act, sim_mm, m - 3)
                ps = p_max[:, :].rearrange("p (c t) -> p c t", c=2 * PAIRS)
                nc.scalar.activation(kT[:, :, WINDOW + b * P:WINDOW + (b + 1) * P], ps[:, PAIRS:2 * PAIRS, :],
                                     ACT.Copy).then_inc(kt_copied, 1)
                for h in range(2):
                    half = slice(h * DH, (h + 1) * DH)
                    nc.scalar.activation(qz[half, b, :, h, :], ps[half, 0:PAIRS, :], ACT.Copy)
                need(act, max_mm, m - 3)
                nc.scalar.activation(qb[:, b, :, :], ps[:, 0:PAIRS, :], ACT.Copy).then_inc(qkt_copied, 1)

            def copy_out(m, b, l, q):
                need(act, ot_mm, m + 1)
                need(act, wo_mm, m - 1)
                nc.scalar.activation(OT[:, b % 2], p_v[:, :].rearrange("p (c t) -> p c t", c=PAIRS), ACT.Copy).then_inc(ot_copied, 1)

            def mlp_copy_input(s, l):
                need(act, m_tr, s + 1)
                nc.scalar.activation(h2[:, :], p_sim[:, 0:512], ACT.Identity, bias=lb[:, l:l + 1],
                                     scale=lg[:, l:l + 1]).then_inc(m_trc, 1)

            def mlp_high(s, l):
                need(act, m_trc, s + 1)
                need(act, up_mm, s * HT)
                nc.scalar.activation(h2T[:, 0, :], h2[:, :], ACT.Copy).then_inc(h2_hi, 1)

            def mlp_gate(s, l, t):
                need(act, up_mm, s * HT + t + 1)
                need(act, hid_done, 2 * s)
                nc.scalar.activation(hg[:, t, :], p_sim[:, 512:1024], ACT.Gelu if t == HT - 1 else ACT.Identity,
                                     bias=b1[:, l, 1, t:t + 1]).then_inc(g_copied, 1)

            def mlp_gelu(s, l):
                need(act, g_copied, s * HT + HT - 1)
                nc.scalar.activation(hg[:, 0:HT - 1, :], hg[:, 0:HT - 1, :], ACT.Gelu).then_inc(gelu_done, 1)

            def input_norm(s):
                need(act, z_nmr, s + 1)
                for c in range(X1_PIECES):
                    if not isinstance(s, int) or X1_SEQS[c] <= s < X1_SEQS[c + 1]:
                        act.wait_ge(x1_out[c], 16)
                for b in range(BLKS):
                    xv = x[:, s * BLKS + b, :]
                    last = nc.scalar.activation(xv, xv, ACT.Identity, bias=znm[:, b:b + 1], scale=zrs[:, b:b + 1])
                last.then_inc(z_done, 1)

            def mlp_norm(s, l):
                need(act, m_nmr, s + 1)
                need(act, m_tr, s)
                for b in range(BLKS):
                    last = nc.scalar.activation(mln[:, b, :], ms[:, b, :], ACT.Identity, bias=mnm[:, b:b + 1],
                                                scale=mrs[:, b:b + 1])
                last.then_inc(m_norm, 1)

            def body(i, layer):
                up = seq_at(i, MLP_UP, layer)
                norm = norm_at(i, layer)
                for b in range(BLKS):
                    def do(step, lag):
                        at = block_at(i, b, lag, layer)
                        if at:
                            step(*at)

                    do(copy_qk, LAG_PROJ)
                    do(square, LAG_PROJ)
                    do(copy_input, LAG_LOAD)
                    if b == 1 and up:
                        mlp_high(*up)
                    do(softmax_exp, LAG_SIM)
                    if b == 2 and norm is not None:
                        input_norm(norm)
                    do(copy_v, LAG_PROJ)
                    if b == BLKS - 1 and up:
                        mlp_gelu(*up)
                    if b == 0 and up:
                        mlp_norm(*up)
                    if b and up:
                        mlp_gate(*up, b - 1)
                    if b == 0 and up:
                        mlp_copy_input(*up)
                    do(copy_qkt, LAG_QKT)
                    do(copy_out, LAG_OT)

            input_norm(0)
            iterate(act, body)

        @block.vector
        def _(dve):
            def table(l, b, part):
                t = tab[:, l, b, part * 2 * DH:(part + 1) * 2 * DH].rearrange("p (k d) -> p k d", k=2)
                return t.unsqueeze(2).broadcast_to([P, 2, HEADS, DH])

            def input_stats(s):
                for b in range(BLKS):
                    nc.vector.bn_stats(zst[:, b, :], x[:, s * BLKS + b, :]).then_inc(z_stats, 1)
                hold(dve, z_stats, s * 2 * BLKS + BLKS)
                for b in range(BLKS):
                    nc.vector.bn_aggr(zmv[:, b, :], zst[:, b, :]).then_inc(z_stats, 1)
                need(dve, z_stats, (s + 1) * 2 * BLKS)
                need(dve, z_done, s)
                nc.vector.tensor_scalar(zrs[:, :], zmv[:, :, 1], EPS, None, ALU.add).then_inc(z_var, 1)

            def input_mean(s):
                need(dve, z_rstd, s + 1)
                nc.vector.scalar_tensor_tensor(znm[:, :], zmv[:, :, 0], -1.0, zrs[:, :], ALU.mult, ALU.mult).then_inc(z_nmr, 1)

            def split_input(m, b, l, q):
                need(dve, ht_hi, m + 1)
                nc.vector.tensor_tensor(hT[:, b % 2, 1, :], p_small[:, 0:P], hT[:, b % 2, 0, :].bitcast(F32),
                                        ALU.subtract).then_inc(ht_copied, 1)

            def mlp_split(s, l):
                need(dve, h2_hi, s + 1)
                nc.vector.tensor_tensor(h2T[:, 1, :], h2[:, :], h2T[:, 0, :].bitcast(F32), ALU.subtract).then_inc(h2_done, 1)

            def copy_maxima(m, b, l, q):
                if isinstance(m, int) and m == 0:
                    dve.wait_ge(init_done, N_INIT)
                need(dve, mt_mm, m + 1)
                need(dve, sim_mm, m - 3)
                nc.vector.tensor_copy(R[ROW_MAX:ROW_MAX + 2 * HEADS, b, :], p_small[0:2 * HEADS, 0:DH].bitcast(BF16)).then_inc(mt_copied, 1)

            def cosine(m, b, l, q):
                need(dve, u_copied, m + 1)
                need(dve, qk_done, m)
                nc.vector.tensor_tensor(t1[:, :].rearrange("p (k h d) -> p k h d", k=2, h=HEADS),
                                        u[:, :].rearrange("p (k h d) -> p k h d", k=2, h=HEADS),
                                        table(l, b, 0), ALU.mult).then_inc(cos_done, 1)

            def sum_squares(m, b, l, q):
                need(dve, squared, m + 1)
                need(dve, rn_done, m - 1)
                nc.vector.tensor_reduce(ss[:, b % 2, :], sq[:, :].rearrange("p (h d) -> p h d", d=DH), AX.X, ALU.add).then_inc(ss_done, 1)
                need(dve, ss_done, m + 1)
                nc.vector.tensor_scalar(ss[:, b % 2, :], ss[:, b % 2, :], NORM_MIN ** 2, None, ALU.max).then_inc(clamped, 1)

            def maxima(m, b, l, q):
                need(dve, max_mm, m + 1)
                need(dve, nm_done, m)
                nc.vector.tensor_reduce(nmax[:, :], p_max[:, :].rearrange("p (h j) -> p h j", h=HEADS), AX.X,
                                        ALU.max, negate=True).then_inc(max_done, 1)
                need(dve, max_done, m + 1)
                need(dve, mt_mm, m - 1)
                nc.vector.tensor_copy(nm2[:, b % 2, 0:HEADS], nmax[:, :]).then_inc(nm_hi, 1)
                need(dve, nm_hi, m + 1)
                nc.vector.tensor_tensor(nm2[:, b % 2, HEADS:2 * HEADS], nmax[:, :], nm2[:, b % 2, 0:HEADS],
                                        ALU.subtract).then_inc(nm_done, 1)

            def add_rotated(m, b, l, q):
                need(dve, cos_done, m + 1)
                need(dve, sin_done, m + 1)
                nc.vector.tensor_tensor(t1[:, :], t1[:, :], t2[:, :], ALU.add).then_inc(rot_done, 1)

            def scale_norms(m, b, l, q):
                need(dve, rot_done, m + 1)
                need(dve, rn_done, m + 1)
                need(dve, qkt_mm, m)
                nc.vector.tensor_tensor(qk[:, :].rearrange("p (h d) -> p h d", d=DH),
                                        t1[:, :].rearrange("p (h d) -> p h d", d=DH),
                                        rn[:, b % 2, :].unsqueeze(2).broadcast_to([P, 2 * HEADS, DH]),
                                        ALU.mult).then_inc(qk_done, 1)

            def normalise_out(m, b, l, q):
                ps = p_qk[:, :].rearrange("p (a c) -> p a c", a=2)[:, :, 0:4 * VW].rearrange("p a (h d) -> p a h d", d=VW)
                need(dve, pv_mm, m + 1)
                need(dve, ot_mm, m - 1)
                need(dve, o_done, m)
                nc.vector.reciprocal(rden[:, :, :], ps[:, :, :, DH]).then_inc(rden_done, 1)
                need(dve, rden_done, m + 1)
                nc.vector.tensor_tensor(O[:, b % 2, :].rearrange("p (a h d) -> p a h d", a=2, h=4), ps[:, :, :, 0:DH],
                                        rden[:, :, :].unsqueeze(3).broadcast_to([P, 2, 4, DH]), ALU.mult).then_inc(o_done, 1)

            def add_attention(m, b, l, q):
                r = row_of(m, l)
                need(dve, wo_mm, m + 1)
                need(dve, ht_mm, capped(m + 2))
                nc.vector.tensor_tensor(x[:, r, :], x[:, r, :], p_small[:, 0:D], ALU.add).then_inc(wo_added, 1)

            def mlp_stats(s, l):
                need(dve, ms_in, 48 * (s + 1))
                for b in range(BLKS):
                    nc.vector.bn_stats(mst[:, b, :], ms[:, b, :]).then_inc(m_stats, 1)
                hold(dve, m_stats, s * 2 * BLKS + BLKS)
                for b in range(BLKS):
                    nc.vector.bn_aggr(mmv[:, b, :], mst[:, b, :]).then_inc(m_stats, 1)
                need(dve, m_stats, (s + 1) * 2 * BLKS)
                need(dve, m_norm, s)
                nc.vector.tensor_scalar(mrs[:, :], mmv[:, :, 1], EPS, None, ALU.add).then_inc(m_var, 1)

            def mlp_mean(s, l):
                need(dve, m_rstd, s + 1)
                nc.vector.scalar_tensor_tensor(mnm[:, :], mmv[:, :, 0], -1.0, mrs[:, :], ALU.mult, ALU.mult).then_inc(m_nmr, 1)

            def mlp_value(s, l, t):
                need(dve, up_mm, s * HT + t + 1)
                need(dve, down_mm, s)
                nc.vector.tensor_scalar(ha[:, t, :], p_sim[:, 0:512], b1[:, l, 0, t:t + 1], None,
                                        ALU.add).then_inc(a_copied, 1)

            def mlp_hidden(s, l, last):
                if last:
                    need(dve, g_copied, (s + 1) * HT)
                    need(dve, a_copied, (s + 1) * HT)
                else:
                    need(dve, gelu_done, s + 1)
                    need(dve, a_copied, s * HT + HT - 1)
                t = slice(HT - 1, HT) if last else slice(0, HT - 1)
                nc.vector.tensor_tensor(ha[:, t, :], ha[:, t, :], hg[:, t, :], ALU.mult).then_inc(hid_done, 1)

            def mlp_add(s, l):
                q = s - l * SEQS
                need(dve, down_mm, s + 1)
                need(dve, b2_added, s + 1)
                xv = x[:, bass.ds(q * BLKS, BLKS), :]
                nc.vector.tensor_tensor(xv, xv, p_sim[:, 512:1024].rearrange("p (b d) -> p b d", b=BLKS),
                                        ALU.add).then_inc(mlp_added, 1)
                if l == LAYERS - 1:
                    need(dve, mlp_added, s + 1)
                    need(dve, x1_in, 16 * (q + 1))
                    nc.vector.tensor_tensor(xv, xv, x1[:, :, :], ALU.add).then_inc(fin_done, 1)

            def body(i, layer):
                up = seq_at(i, MLP_UP, layer)
                down = seq_at(i, MLP_DOWN, layer)
                norm = norm_at(i, layer)
                for b in range(BLKS):
                    def do(step, lag):
                        at = block_at(i, b, lag, layer)
                        if at:
                            step(*at)

                    if b == 2 and norm is not None:
                        input_mean(norm)
                    do(scale_norms, LAG_SCALE)
                    if b == 0 and up:
                        mlp_stats(*up)
                    if b == 0 and down:
                        mlp_hidden(*down, True)
                    if b == 1 and norm is not None:
                        input_stats(norm)
                    do(cosine, LAG_PROJ)
                    if b == 0 and up:
                        mlp_mean(*up)
                    do(split_input, LAG_LOAD)
                    do(sum_squares, LAG_PROJ)
                    if b == 1 and up:
                        mlp_split(*up)
                    do(maxima, LAG_MAX)
                    do(normalise_out, LAG_PV)
                    do(add_attention, LAG_WO)
                    if b == 0 and down:
                        mlp_add(*down)
                    do(add_rotated, LAG_PROJ)
                    do(copy_maxima, LAG_MAX)
                    if b and up:
                        mlp_value(*up, b - 1)
                    if b == BLKS - 1 and up:
                        mlp_hidden(*up, False)

            input_stats(0)
            input_mean(0)
            iterate(dve, body)

        @block.gpsimd
        def _(pool):
            pool.memset(xs[0:1, 0, DH:D], 0.0).then_inc(init_done, 1)
            pool.memset(ms[0:1, 0, DH:D], 0.0).then_inc(init_done, 1)
            pool.memset(Vs[0:DH, 0, :, :], 0.0).then_inc(init_done, 1)
            pool.memset(V[:, :, :, DH:VW], 1.0).then_inc(init_done, 1)
            pool.memset(minus_half[:, :], -0.5).then_inc(init_done, 1)
            pool.wait_ge(init_done, N_INIT_DMA + 1)

            def input_rstd(s):
                need(pool, z_var, s + 1)
                nc.gpsimd.tensor_tensor(zrs[:, :], zrs[:, :], minus_half[:, 0:BLKS], ALU.pow).then_inc(z_rstd, 1)

            input_rstd(0)
            pool.memset(R[:, :, :], 0.0).then_inc(init_done, 1)
            pool.memset(qz[:, :, :, :, :], 0.0).then_inc(init_done, 1)
            pool.memset(kT[:, :, 0:WINDOW], 0.0).then_inc(init_done, 1)
            pool.memset(kzb[:, :, :, :], 0.0).then_inc(init_done, 1)
            pool.wait_ge(init_done, N_INIT - 3)
            for v in range(2):
                nc.gpsimd.tensor_copy(R[0:WINDOW, :, v * WINDOW:(v + 1) * WINDOW],
                                      identb[0:WINDOW, 0:WINDOW].unsqueeze(1).broadcast_to([WINDOW, BLKS, WINDOW])).then_inc(init_done, 1)
            pool.memset(R[ROW_FIRST:ROW_FIRST + 1, 0, 0:WINDOW], 1.0).then_inc(init_done, 1)
            pool.wait_ge(init_done, N_INIT)

            def sine(m, b, l, q):
                need(pool, u_copied, m + 1)
                need(pool, rot_done, m)
                half = DH // 2
                src = u[:, :].rearrange("p (h a d) -> p h a d", a=2, d=half)
                dst = t2[:, :].rearrange("p (h a d) -> p h a d", a=2, d=half)
                for k in range(2):
                    t = tab[:, l, b, (2 + k) * DH:(3 + k) * DH].rearrange("p (a d) -> p a d", a=2)
                    heads = slice(k * HEADS, (k + 1) * HEADS)
                    for a in range(2):
                        last = nc.gpsimd.tensor_tensor(dst[:, heads, a, :], src[:, heads, 1 - a, :],
                                                       t[:, a, :].unsqueeze(1).broadcast_to([P, HEADS, half]), ALU.mult)
                last.then_inc(sin_done, 1)

            def to_bf16(m, b, l, q):
                need(pool, kt_copied, m + 1)
                hold(pool, max_mm, m - 3)
                cols = slice(WINDOW + b * P, WINDOW + (b + 1) * P)
                for h in range(2):
                    last = nc.gpsimd.tensor_scalar(kzb[:, :, h, cols], kT[:, :, cols], halves[:, h:h + 1], 0.0, ALU.mult, ALU.add)
                last.then_inc(bf_done, 1)

            def norms(m, b, l, q):
                need(pool, clamped, m + 1)
                need(pool, qk_done, m - 1)
                nc.gpsimd.tensor_tensor(rn[:, b % 2, :], ss[:, b % 2, :], minus_half[:, :], ALU.pow).then_inc(rn_done, 1)

            def mlp_rstd(s, l):
                need(pool, m_var, s + 1)
                nc.gpsimd.tensor_tensor(mrs[:, :], mrs[:, :], minus_half[:, 0:BLKS], ALU.pow).then_inc(m_rstd, 1)

            def add_b2(s, l):
                q = s - l * SEQS
                need(pool, ms_in, 48 * (s + 1))
                xv = x[:, bass.ds(q * BLKS, BLKS), :]
                nc.gpsimd.tensor_tensor(xv, xv, b2[:, l, :].unsqueeze(1).broadcast_to([P, BLKS, D]), ALU.add).then_inc(b2_added, 1)

            def body(i, layer):
                up = seq_at(i, MLP_UP, layer)
                norm = norm_at(i, layer)
                for b in range(BLKS):
                    if b == 0 and up:
                        mlp_rstd(*up)
                    if b == 1 and norm is not None:
                        input_rstd(norm)
                    at = block_at(i, b, LAG_PROJ, layer)
                    if at:
                        sine(*at)
                        norms(*at)
                    if b == 1 and up:
                        add_b2(*up)
                    at = block_at(i, b, LAG_QKT, layer)
                    if at:
                        to_bf16(*at)

            iterate(pool, body)


N_STAGED = 9
N_INIT_DMA = 4
N_INIT = 12


def ema_then_stack(nc, T):
    with ExitStack() as ctx:
        W = stack_weights(nc, ctx)
        T["taps"] = nc.dram_tensor("taps_dram", [P, 2 * P], F32, kind="Internal").ap()
        T["x1"] = nc.dram_tensor("x1_dram", [SEQS, LEN, D], F32, kind="Internal").ap()
        ema_part(nc, T, W)
        stack_part(nc, T, W)


def shape_constants(np, bf16):
    f = np.float32
    half = np.arange(0, DH, 2, dtype=f)
    inv = (f(1.0) / f(10000.0) ** (half / f(DH))).astype(f)
    t = np.arange(LEN, dtype=f)
    fr = (t[:, None] * inv[None, :]).astype(f).astype(np.float64)
    fr = np.concatenate([fr, fr], 1)
    base = ((half + f(0.4 * DH)) / f(1.4 * DH)).astype(f)
    power = ((t - LEN // 2) / f(WINDOW // 2)).astype(f)
    sc = base.astype(np.float64)[None, :] ** power.astype(np.float64)[:, None]
    sc = np.concatenate([sc, sc], 1)
    sign = np.where(np.arange(DH) < DH // 2, -1.0, 1.0)
    rope = np.stack([QK_SCALE * np.cos(fr) * sc, np.cos(fr) / sc,
                     QK_SCALE * np.sin(fr) * sc * sign, np.sin(fr) / sc * sign], 1)
    rope = rope.reshape(BLKS, P, 4 * DH).transpose(1, 0, 2).astype(f)
    q = np.arange(P)[:, None] % WINDOW
    j = np.arange(P)[None, :]
    band = np.where((j < q) | (j > q + WINDOW), NEG, 0.0)
    first = np.where((np.arange(P)[:, None] < WINDOW) & (j < WINDOW), NEG, 0.0)
    mask_n = np.stack([band, band + first], 1).astype(bf16)
    mask_t = np.zeros((P, HEADS, P))
    mask_t[0:WINDOW] = band[0:WINDOW][:, None, :]
    for h in range(HEADS):
        mask_t[ROW_MAX + h, h] = 1.0
        mask_t[ROW_MAX + HEADS + h, h] = 1.0
    mask_t[ROW_FIRST, :, 0:WINDOW] = NEG
    ramp = np.concatenate([np.tile(np.arange(P), (P, 1)), np.tile(np.arange(1, P + 1), (P, 1)),
                           np.arange(P)[:, None]], 1).astype(f)
    return {"rope": np.ascontiguousarray(rope), "mask_n": mask_n, "mask_t": mask_t.astype(bf16),
            "ident": np.eye(P, dtype=f),
            "halves": np.repeat(np.eye(2, dtype=f), DH, 0), "identb": np.eye(P).astype(bf16), "ramp": ramp}


_ATTN = {"x": "x", "delta": "delta", "alpha": "alpha", "beta": "beta", "gamma": "gamma", "omega": "omega"}
_FFN = ["wqkv", "q_scale", "k_scale", "wo", "ln_g", "ln_b", "w1", "b1", "w2", "b2"]


def kernel(**inputs):
    import ml_dtypes
    import numpy as np
    import concourse.bacc as bacc
    from concourse.bass_utils import run_bass_kernel_spmd

    arrays = {name: np.ascontiguousarray(inputs[f"L0_attn_{name}"]) for name in _ATTN}
    for name in ("delta", "alpha", "beta"):
        arrays[name] = arrays[name].reshape(D, STATES)
    arrays["x_rev"] = np.ascontiguousarray(arrays["x"].reshape(SEQS, BLKS, P, D)[:, :, ::-1]).reshape(SEQS, LEN, D)
    arrays.update({name: np.ascontiguousarray(inputs[f"L0_ffn_{name}"]) for name in _FFN})
    for name in ("delta", "alpha", "beta", "gamma", "ln_g", "ln_b"):
        arrays[name + "_t"] = np.ascontiguousarray(arrays[name].T)
    b1 = np.zeros((LAYERS, 2, HT * P), arrays["b1"].dtype)
    b1[:, :, :HID] = arrays.pop("b1").reshape(LAYERS, 2, HID)
    arrays["b1_t"] = np.ascontiguousarray(b1.reshape(LAYERS, 2, HT, P).transpose(3, 0, 1, 2))
    arrays.update(shape_constants(np, ml_dtypes.bfloat16))
    nc = bacc.Bacc("TRN2", target_bir_lowering=False, num_devices=1)
    feed, T = {}, {}
    for name, a in arrays.items():
        feed[f"in_{name}_dram"] = a
        T[name] = nc.dram_tensor(f"in_{name}_dram", a.shape, mybir.dt.from_np(a.dtype), kind="ExternalInput").ap()
    T["out"] = nc.dram_tensor("out_dram", (SEQS, LEN, D), F32, kind="ExternalOutput").ap()
    ema_then_stack(nc, T)
    return run_bass_kernel_spmd(nc, [feed], core_ids=[0]).results[0]["out_dram"]
```
